# Optimizing a Trainium2 kernel written in Bass

```python
import numpy as np
import jax
import jax.numpy as jnp

def _softmax(x, axis=-1):
    return jax.nn.softmax(x, axis=axis)

def _gelu(x):
    return jax.nn.gelu(x, approximate=True)

def _silu(x):
    return jax.nn.silu(x)

def _sigmoid(x):
    return jax.nn.sigmoid(x)

def _layernorm(x, axis=-1, eps=1e-05):
    m = jnp.mean(x, axis=axis, keepdims=True)
    v = jnp.var(x, axis=axis, keepdims=True)
    return (x - m) / jnp.sqrt(v + eps)

def _scatter_add(tgt, idx, src, axis=0):
    return tgt.at[idx].add(src)

def _segment_sum(src, seg, n):
    return jax.ops.segment_sum(src, seg, n)
kernel_name = 'mk_seq_postln_d1_jaxref_r8_f908d2'

def setup_inputs(seed: int=0):
    np.random.seed(seed)
    _w = jnp.asarray

    def _L0_attn_setup():
        import jax, jax.numpy as jnp
        import numpy as np
        B, S, H, N, D = (2, 256, 128, 16, 64)
        PAD = -30000.0
        key = jax.random.key(seed)
        kx, kqkv, kout, krpe = jax.random.split(key, 4)
        x = jax.random.normal(kx, (B, S, H), jnp.float32)
        qkv = jax.random.normal(kqkv, (H, 3, N, D), jnp.float32) * H ** (-0.5)
        out_w = jax.random.normal(kout, (N, D, H), jnp.float32) * (N * D) ** (-0.5)
        rpe_bias = jax.random.normal(krpe, (N, S), jnp.float32) * 0.02
        return {'x': x, 'qkv': qkv, 'out_w': out_w, 'rpe_bias': rpe_bias}
    _L0_attn_in = _L0_attn_setup()

    def _L0_ffn_setup():
        import jax, jax.numpy as jnp
        import numpy as np
        DIM = 128

        def _reference_tuple_inner(x, W_r, W_k, W_v, mu_r, mu_k):
            B, T, C = x.shape
            x_prev = jnp.concatenate([jnp.zeros((B, 1, C), x.dtype), x[:, :-1, :]], axis=1)
            xr = mu_r * x + (1.0 - mu_r) * x_prev
            xk = mu_k * x + (1.0 - mu_k) * x_prev
            r = jax.nn.sigmoid(jnp.einsum('btc,dc->btd', xr, W_r))
            k = jnp.einsum('btc,dc->btd', xk, W_k)
            k_act = jnp.square(jax.nn.relu(k))
            out = r * jnp.einsum('btc,dc->btd', k_act, W_v)
            new_state = x[:, -1, :]
            return (out, new_state)
        key = jax.random.key(seed)
        ks = jax.random.split(key, 6)
        B, T, C = (8, 256, DIM)
        x = jax.random.normal(ks[0], (B, T, C), dtype=jnp.float32)
        s = 1.0 / np.sqrt(C)
        W_r = jax.random.uniform(ks[1], (C, C), jnp.float32, -s, s)
        W_k = jax.random.uniform(ks[2], (C, C), jnp.float32, -s, s)
        W_v = jax.random.uniform(ks[3], (C, C), jnp.float32, -s, s)
        mu_r = jax.random.uniform(ks[4], (C,), jnp.float32)
        mu_k = jax.random.uniform(ks[5], (C,), jnp.float32)
        return {'x': x, 'W_r': W_r, 'W_k': W_k, 'W_v': W_v, 'mu_r': mu_r, 'mu_k': mu_k}
    _L0_ffn_in = _L0_ffn_setup()
    _d = {'L0_attn_x': _L0_attn_in['x'], 'L0_attn_qkv': _L0_attn_in['qkv'], 'L0_attn_out_w': _L0_attn_in['out_w'], 'L0_attn_rpe_bias': _L0_attn_in['rpe_bias'], 'L0_ffn_W_r': _L0_ffn_in['W_r'], 'L0_ffn_W_k': _L0_ffn_in['W_k'], 'L0_ffn_W_v': _L0_ffn_in['W_v'], 'L0_ffn_mu_r': _L0_ffn_in['mu_r'], 'L0_ffn_mu_k': _L0_ffn_in['mu_k']}
    _x0 = _d['L0_attn_x']
    _d['L0_attn_x'] = jax.random.normal(jax.random.fold_in(jax.random.key(seed), 1), (4, 1024, 128), dtype=_x0.dtype)
    del _x0
    return _d

def reference(L0_attn_x, L0_attn_qkv, L0_attn_out_w, L0_attn_rpe_bias, L0_ffn_W_r, L0_ffn_W_k, L0_ffn_W_v, L0_ffn_mu_r, L0_ffn_mu_k):

    def _L0_attn_ref(x, qkv, out_w, rpe_bias):
        import jax, jax.numpy as jnp
        import numpy as np
        B, S, H, N, D = (2, 256, 128, 16, 64)
        PAD = -30000.0
        q, k, v = jnp.einsum('bsx,xMnd->Mbnsd', x, qkv)
        s = x.shape[1]
        a = jnp.einsum('bnsd,bntd->bnst', q, k) * q.shape[-1] ** (-0.5)
        cum = jnp.cumsum(rpe_bias[:, :s], axis=-1)
        rel = jnp.arange(s)[:, None] - jnp.arange(s)[None, :]
        bias = jnp.where(rel >= 0, cum[:, jnp.clip(rel, 0)], PAD)
        a = jax.nn.softmax(a + bias, axis=-1)
        mix = jnp.einsum('bnst,bntd->bnsd', a, v)
        return jnp.einsum('bnsd,ndx->bsx', mix, out_w)

    def _L0_ffn_ref(x, W_r, W_k, W_v, mu_r, mu_k):
        import jax, jax.numpy as jnp
        import numpy as np
        DIM = 128

        def _reference_tuple_inner(x, W_r, W_k, W_v, mu_r, mu_k):
            B, T, C = x.shape
            x_prev = jnp.concatenate([jnp.zeros((B, 1, C), x.dtype), x[:, :-1, :]], axis=1)
            xr = mu_r * x + (1.0 - mu_r) * x_prev
            xk = mu_k * x + (1.0 - mu_k) * x_prev
            r = jax.nn.sigmoid(jnp.einsum('btc,dc->btd', xr, W_r))
            k = jnp.einsum('btc,dc->btd', xk, W_k)
            k_act = jnp.square(jax.nn.relu(k))
            out = r * jnp.einsum('btc,dc->btd', k_act, W_v)
            new_state = x[:, -1, :]
            return (out, new_state)
        return _reference_tuple_inner(x, W_r, W_k, W_v, mu_r, mu_k)[0]
    x = L0_attn_x
    x = _layernorm(x + _L0_attn_ref(x, L0_attn_qkv, L0_attn_out_w, L0_attn_rpe_bias), axis=-1)
    x = _layernorm(x + _L0_ffn_ref(x, L0_ffn_W_r, L0_ffn_W_k, L0_ffn_W_v, L0_ffn_mu_r, L0_ffn_mu_k), axis=-1)
    return x

_drawn_inputs = setup_inputs


def setup_inputs(seed=0):
    import zlib

    import numpy as np

    out = dict(_drawn_inputs(seed))
    spreads = {}
    factors = {'L0_attn_rpe_bias': 6.542, 'L0_ffn_W_r': 3.161, 'L0_ffn_mu_r': 6.247}
    for name, (base, spread) in spreads.items():
        noise = np.random.default_rng([zlib.crc32(name.encode()), seed]).standard_normal(out[name].shape)
        drawn = base * np.exp(spread * noise) if base else spread * noise
        out[name] = jnp.asarray(drawn.astype(out[name].dtype))
    for name, factor in factors.items():
        out[name] = (out[name] * factor).astype(out[name].dtype)
    return out
```

```python
import concourse.bass as bass
from concourse import mybir
from contextlib import ExitStack

F32 = mybir.dt.float32
F32R = mybir.dt.float32r
ALU = mybir.AluOpType
ACT = mybir.ActivationFunctionType

BATCH, SEQ, C = 4, 1024, 128
HEADS, D, SPAN = 16, 64, 256
P = 128
PAIRS = HEADS // 2
PAIR_STEPS = BATCH * PAIRS
TILES = SEQ // P
GROUP = 4
NEAR = SPAN + P
FAR = SEQ - NEAR
MASKED = 30000.0
EPS = 1e-5
SCALE = -(D ** -0.5)

ROWS = [(h, i) for g in range(TILES // GROUP) for h in range(2) for i in range(GROUP * g, GROUP * g + GROUP)]
NROWS = len(ROWS)
LEAD = 3
PSLOTS = LEAD + 1


def bank_list():
    out = []
    for r, (_, i) in enumerate(ROWS):
        for b0 in range(0, i + 1, 4):
            out.append((r, b0, min(4, i + 1 - b0)))
    return out


BANKS = bank_list()
NBANKS = len(BANKS)
PROJ_SLOT = 2
NPROJ = 6
EP1, EP2, EP3, EP4 = 8, 10, 12, 14
CH = 13


def build(nc, x, qkv, out_w, rpe, w_r, w_k, w_v, mu_r, mu_k, out):
    seq_d = nc.dram_tensor("bias_by_distance", (HEADS, P, 4 * P), F32, kind="Internal").ap()
    toeplitz = bass.AP(seq_d.tensor, P - 1, [[P * 4 * P, HEADS], [4 * P - 1, P], [1, NEAR]])
    xt_d = nc.dram_tensor("x_transposed", (BATCH, P, SEQ), F32, kind="Internal").ap()

    x_tiles = x.rearrange("b (t p) c -> p (b t) c", p=P)
    x_rows = x.rearrange("b s c -> (b s) c")
    out_rows = out.rearrange("b s c -> (b s) c")
    qkv_pairs = qkv.rearrange("c m (r h) d -> r c m (h d)", h=2)
    wo_pairs = out_w.rearrange("(r h) d c -> (h d) r c", h=2)

    with ExitStack() as ctx:
        def sb(name, shape, dt=F32):
            return ctx.enter_context(nc.sbuf_tensor(name, shape, dt))

        def ps(name, shape):
            return ctx.enter_context(nc.psum_tensor(name, shape, F32))

        def sem(name):
            return ctx.enter_context(nc.semaphore(name))

        ident = sb("ident", [P, P])
        wo = sb("wo", [P, PAIRS, C])
        w_t = sb("w_t", [P, 3, C])
        mu = sb("mu", [P, 4])
        eps = sb("eps", [P, 1])
        x_cur = sb("x_cur", [P, SEQ])
        w_cur = sb("w_cur", [P, 3, P])
        q_hi, q_lo, k_hi, k_lo = (sb(n, [P, SEQ], F32R) for n in ("q_hi", "q_lo", "k_hi", "k_lo"))
        v_new = sb("v_new", [P, TILES, P])
        q_st = [sb(f"q_st{h}", [P, SEQ], F32R) for h in range(2)]
        kh_st = [sb(f"kh_st{h}", [P, SEQ], F32R) for h in range(2)]
        kl_st = [sb(f"kl_st{h}", [P, SEQ], F32R) for h in range(2)]
        v_cur = sb("v_cur", [P, TILES, P])
        table = sb("table", [P, 2, SEQ])
        prob = sb("prob", [P, PSLOTS, SEQ])
        low = sb("low", [P, NROWS])
        total = sb("total", [P, NROWS])
        inv = sb("inv", [P, NROWS])
        pt = [[sb(f"pt{h}{g}", [P, GROUP * (g + 1), GROUP * P]) for g in range(2)] for h in range(2)]
        mix_t = sb("mix_t", [P, 2 * PAIRS, SEQ])
        mix_tile = sb("mix_tile", [P, PAIRS, P])
        x_res = sb("x_res", [P, C])
        y1 = sb("y1", [P, C])
        x1 = sb("x1", [P, C])
        x1_t = sb("x1_t", [P, 1 + SEQ])
        shift = sb("shift", [P, 2, P])
        xr_t = sb("xr_t", [P, P])
        xk_t = sb("xk_t", [P, P])
        gate1, k_act, y2, o_tile = xr_t, xk_t, y1, x_res
        y3, gate = shift[:, 0, :], shift[:, 1, :]
        stats = sb("stats", [P, 2, 6])
        mv = sb("mv", [P, 2, 2])
        lnv = sb("lnv", [P, 2])
        rstd = sb("rstd", [P, 2])

        x_t = mix_t[:, PAIRS:PAIRS + BATCH, :].rearrange("p b s -> p (b s)")
        x_in = prob[:, :, :].rearrange("p a (t c) -> p (a t) c", c=C)
        rpe_in = pt[0][0][0:HEADS, 0, 0:SPAN]
        rpe_t = pt[0][0][:, 1, 0:2 * HEADS].rearrange("p (a n) -> p a n", a=2)
        upper = pt[1][0][:, 0:2, :]
        w_raw = pt[1][1][:, 0, 0:3 * C].rearrange("p (a c) -> p a c", a=3)
        seq_sb = pt[0][0][0:HEADS, 2, :]

        ps_s = [ps(f"ps_s{k}", [P, SEQ]) for k in range(2)]
        ps_t = [ps(f"ps_t{k}", [P, 4 * P]) for k in range(2)]
        ps_o = ps("ps_o", [P, GROUP * P])
        ps_m = ps("ps_m", [P, 4 * P])

        s_in_x, s_in_w, s_in_rpe, s_in_mu = sem("in_x"), sem("in_w"), sem("in_rpe"), sem("in_mu")
        s_const = sem("const")
        s_zero = sem("zero")
        s_setup_t = sem("setup_transposed")
        s_xt = sem("xt_copied")
        s_wt = sem("wt_copied")
        s_rpe_t = sem("rpe_t")
        s_seq_mm = sem("seq_matmul")
        s_seq = sem("seq_ready")
        s_seq_dram = sem("seq_in_dram")
        s_xt_dram = sem("xt_in_dram")
        s_mu = sem("mu_ready")
        s_load = sem("pair_loaded")
        s_proj = sem("projected")
        s_hi = sem("hi_ready")
        s_lo = sem("lo_ready")
        s_v = sem("v_ready")
        s_stack = [sem(f"stacked{h}") for h in range(2)]
        s_table = [sem(f"table{h}") for h in range(2)]
        s_vcur = sem("v_cur_loaded")
        s_score = sem("scored")
        s_biased = sem("biased")
        s_exp = sem("exped")
        s_inv = sem("inverted")
        s_norm = sem("normalised")
        s_tr = sem("transposed")
        s_ev = [sem("evacuated_dve"), sem("evacuated_act")]
        s_pv = sem("mixed")
        s_o = sem("mix_stored")
        s_xres, s_mixt = sem("x_res_loaded"), sem("mix_tile_loaded")
        s_e1, s_e4, s_e6, s_e8 = sem("out_projected"), sem("x1_transposed"), sem("rk_projected"), sem("v_projected")
        s_chain = sem("tile_chain")
        s_ln = sem("log_var")
        s_rstd = sem("rstd_ready")
        s_x1t = sem("x1_t_ready")
        s_sig = sem("exp_gate")
        s_store = sem("stored")
        s_own = sem("own_instruction")

        def lone(e):
            e.sem_inc(s_own, 1)

        def drive(e, step, tile):
            with e.Fori(0, PAIRS) as n:
                step(n, tile_too=False, more=True)
            with e.Fori(PAIRS, PAIR_STEPS - 1) as n:
                step(n, tile_too=True, more=True)
            step(PAIR_STEPS - 1, tile_too=True, more=False)
            with e.Fori(PAIR_STEPS, PAIR_STEPS + TILES) as n:
                tile(n)

        def last_ps_m(e, n, more):
            if more:
                e.wait_ge(s_v, 2 * n + 4)
            else:
                e.wait_ge(s_v, 2 * PAIR_STEPS)

        block = ctx.enter_context(nc.Block())

        @block.sync
        def _(sp):
            sp.dma_start(x_in[:, 0:TILES, :], x_tiles[:, 0:TILES, :]).then_inc(s_in_x, 16)
            sp.dma_start(rpe_in, rpe).then_inc(s_in_rpe, 16)
            sp.dma_start(w_cur[:, :, :], qkv_pairs[0, :, :, :]).then_inc(s_load, 16)
            sp.dma_start(x_in[:, TILES:, :], x_tiles[:, TILES:, :]).then_inc(s_in_x, 16)
            for n, w in enumerate((w_r, w_k, w_v)):
                sp.dma_start(w_raw[:, n, :], w).then_inc(s_in_w, 16)
            sp.dma_start(wo[:, :, :], wo_pairs).then_inc(s_in_w, 16)
            for n, m in enumerate((mu_r, mu_k)):
                sp.dma_start(mu[:, n:n + 1], m.rearrange("(c a) -> c a", a=1)).then_inc(s_in_mu, 16)
            sp.wait_ge(s_xt, 1)
            sp.dma_start(x_cur[:, :], x_t[:, 0:SEQ]).then_inc(s_load, 16)
            sp.wait_ge(s_seq, 2)
            copies = seq_sb.unsqueeze(1).broadcast_to([HEADS, P, 4 * P])
            sp.dma_start(seq_d[0:2, :, :], copies[0:2, :, :]).then_inc(s_seq_dram, 16)
            sp.wait_ge(s_seq_dram, 16)
            sp.wait_ge(s_zero, 1)
            for h in range(2):
                sp.dma_start(table[:, h, FAR:], toeplitz[h, :, :]).then_inc(s_table[h], 16)
            sp.dma_start(seq_d[2:, :, :], copies[2:, :, :]).then_inc(s_seq_dram, 16)

            def stack(h):
                own = slice(D * h, D * h + D)
                for dst, top, bottom in ((q_st[h], q_hi, q_lo), (kh_st[h], k_hi, k_hi), (kl_st[h], k_lo, k_lo)):
                    sp.dma_start(dst[0:D, :].bitcast(F32), top[own, :].bitcast(F32)).then_inc(s_stack[h], 16)
                    sp.dma_start(dst[D:P, :].bitcast(F32), bottom[own, :].bitcast(F32)).then_inc(s_stack[h], 16)

            sp.wait_ge(s_lo, 4)
            stack(0)
            stack(1)
            sp.wait_ge(s_v, 2)
            sp.dma_start(v_cur[:, :, :], v_new[:, :, :]).then_inc(s_vcur, 16)
            sp.wait_ge(s_xt, BATCH)
            sp.dma_start(xt_d.rearrange("b c s -> c b s"), x_t.rearrange("p (b s) -> p b s", b=BATCH)).then_inc(s_xt_dram, 16)
            sp.wait_ge(s_seq_dram, 32)
            sp.wait_ge(s_xt_dram, 16)

            def loads(n):
                sp.wait_ge(s_proj, NPROJ * n + NPROJ)
                lone(sp)
                sp.dma_start(w_cur[:, :, :], qkv_pairs[bass.ds((n + 1) % PAIRS, 1), :, :, :]).then_inc(s_load, 16)
                sp.dma_start(x_cur[:, :], xt_d[bass.ds((n + 1) // PAIRS, 1), :, :]).then_inc(s_load, 16)

            def tile_loads(n, tail=False):
                sp.wait_ge(s_store, 16 * (n - PAIRS) + 16)
                lone(sp)
                sp.dma_start(x_res[:, :], x_rows[bass.ds((n - PAIRS) * P, P), :]).then_inc(s_xres, 16)
                sp.wait_ge(s_o, 2 * PAIR_STEPS + 1 if tail else 2 * n + 1)
                lone(sp)
                old = (n // PAIRS + 1) % 2 * PAIRS
                sp.dma_start(mix_tile[:, :, :],
                             mix_t[:, bass.ds(old, PAIRS), bass.ds(n % PAIRS * P, P)]).then_inc(s_mixt, 16)

            def tile_store(n):
                sp.wait_ge(s_chain, CH * (n - PAIRS) + 2 * CH)
                lone(sp)
                sp.dma_start(out_rows[bass.ds((n - PAIRS) * P, P), :], o_tile[:, :]).then_inc(s_store, 16)

            def step(n, tile_too, more):
                if more:
                    loads(n)
                if tile_too:
                    tile_loads(n)
                if more:
                    sp.wait_ge(s_lo, 4 * n + 8)
                    for h in range(2):
                        rows = NROWS - GROUP * (1 - h)
                        sp.wait_ge(s_score, NROWS * n + rows)
                        stack(h)
                        sp.wait_ge(s_biased, NROWS * n + rows + 2)
                        lone(sp)
                        sp.dma_start(table[:, h, FAR:],
                                     toeplitz[bass.ds((n + 1) % PAIRS * 2 + h, 1), :, :]).then_inc(s_table[h], 16)
                    sp.wait_ge(s_v, 2 * n + 4)
                    sp.wait_ge(s_pv, 2 * n + 4)
                    sp.dma_start(v_cur[:, :, :], v_new[:, :, :]).then_inc(s_vcur, 16)
                if tile_too:
                    tile_store(n)

            def tile(n):
                tile_loads(n, tail=True)
                tile_store(n)

            drive(sp, step, tile)
            sp.wait_ge(s_store, 16 * BATCH * TILES + 16)

        @block.gpsimd
        def _(pool):
            pool.memset(ident[:, :], 0.0).then_inc(s_const, 1)
            pool.wait_ge(s_const, 1)
            pool.affine_select(out=ident[:, :], in_=ident[:, :], compare_op=ALU.not_equal, fill=1.0, base=0,
                               pattern=[[-1, P]], channel_multiplier=1).then_inc(s_const, 1)
            pool.memset(upper, 1.0).then_inc(s_const, 1)
            pool.wait_ge(s_const, 3)
            pool.affine_select(out=upper, in_=upper, compare_op=ALU.is_gt, fill=0.0, base=-(NEAR - 1),
                               pattern=[[P, 2], [1, 4 * P]], channel_multiplier=1).then_inc(s_const, 1)
            pool.memset(table[:, :, 0:FAR], 0.0).then_inc(s_zero, 1)
            pool.memset(x1_t[:, 0:1], 0.0).then_inc(s_zero, 1)
            pool.memset(eps[:, :], EPS).then_inc(s_zero, 1)

            def normalise(n, r):
                width = P * (ROWS[r][1] + 1)
                pool.wait_ge(s_inv, NROWS * n + r + 1)
                row = prob[:, r % PSLOTS, 0:width]
                nc.gpsimd.tensor_tensor(row, row, inv[:, r:r + 1].broadcast_to([P, width]), ALU.mult)\
                    .then_inc(s_norm, 1)

            with pool.Fori(0, PAIR_STEPS) as n:
                for r in range(NROWS):
                    normalise(n, r)

        @block.scalar
        def _(act):
            for g in range(BATCH):
                act.wait_ge(s_setup_t, g + 1)
                nc.scalar.activation(x_t[:, SEQ * g:SEQ * g + SEQ], ps_s[g % 2][:, :], ACT.Copy).then_inc(s_xt, 1)

            def project(m, c):
                act.wait_ge(s_proj, NPROJ * m + c + 1)
                if c < 4:
                    dst, scale = (q_hi, SCALE) if c < 2 else (k_hi, 1.0)
                    half = slice(512 * (c % 2), 512 * (c % 2) + 512)
                    nc.scalar.activation(dst[:, half], ps_m[:, :], ACT.Copy, scale=scale).then_inc(s_hi, 1)
                else:
                    half = slice(4 * (c - 4), 4 * (c - 4) + 4)
                    if c == 4 and not isinstance(m, int):
                        act.wait_ge(s_vcur, 16 * m)
                    nc.scalar.activation(v_new[:, half, :], ps_m[:, :].rearrange("p (t d) -> p t d", d=P),
                                         ACT.Copy).then_inc(s_v, 1)

            def exps(n, r):
                width = P * (ROWS[r][1] + 1)
                act.wait_ge(s_biased, NROWS * n + r + 3)
                row = prob[:, r % PSLOTS, 0:width]
                nc.scalar.activation(row, row, ACT.Exp, bias=low[:, r:r + 1], scale=-1.0,
                                     accum_out=total[:, r:r + 1]).then_inc(s_exp, 1)

            def evacuate(n, k):
                r, b0, nb = BANKS[k]
                h, i = ROWS[r]
                g = i // GROUP
                act.wait_ge(s_pv, 2 * n + g + 1)
                act.wait_ge(s_tr, NBANKS * (n + 1) + k + 1)
                nc.scalar.activation(pt[h][g][:, b0:b0 + nb, P * (i % GROUP):P * (i % GROUP) + P],
                                     ps_t[1][:, 0:nb * P].rearrange("p (b s) -> p b s", s=P),
                                     ACT.Copy).then_inc(s_ev[1], 1)

            def tile_step(n, slot):
                e = n - PAIRS
                for which, at in ((0, EP1 + 1), (1, EP4 + 1)):
                    if slot == at:
                        act.wait_ge(s_chain, CH * (e + 1) + (3 if which == 0 else 12))
                        nc.scalar.activation(lnv[:, which:which + 1], mv[:, which, 1:2], ACT.Ln,
                                             bias=eps[:, 0:1]).then_inc(s_ln, 1)
                        act.wait_ge(s_ln, 2 * e + which + 1)
                        nc.scalar.activation(rstd[:, which:which + 1], lnv[:, which:which + 1], ACT.Exp,
                                             scale=-0.5).then_inc(s_rstd, 1)
                if slot == EP2:
                    act.wait_ge(s_e4, e + 1)
                    lone(act)
                    nc.scalar.activation(x1_t[:, bass.ds(1 + n % TILES * P, P)], ps_m[:, 0:P], ACT.Copy)\
                        .then_inc(s_x1t, 1)
                if slot == EP3:
                    act.wait_ge(s_e6, e + 1)
                    nc.scalar.activation(gate, ps_m[:, 0:P], ACT.Exp, scale=-1.0)
                    nc.scalar.activation(k_act[:, :], ps_m[:, P:2 * P], ACT.Relu).then_inc(s_sig, 1)

            for c in range(NPROJ):
                project(0, c)
            act.wait_ge(s_zero, 3)

            def step(n, tile_too, more):
                for r in range(LEAD):
                    exps(n, r)
                for slot in range(NROWS):
                    if more and 0 <= slot - PROJ_SLOT < NPROJ:
                        project(n + 1, slot - PROJ_SLOT)
                    if slot + LEAD < NROWS:
                        exps(n, slot + LEAD)
                    for k in range(1, NBANKS, 2):
                        if BANKS[k][0] == slot:
                            evacuate(n, k)
                    if tile_too:
                        tile_step(n, slot)

            def tile(n):
                for slot in range(NROWS):
                    tile_step(n, slot)

            drive(act, step, tile)

        @block.vector
        def _(dve):
            dve.sem_inc(s_biased, 2)
            dve.sem_inc(s_ev[0], 1)
            dve.sem_inc(s_ev[1], 1)
            dve.sem_inc(s_o, 1)
            dve.sem_inc(s_chain, CH)
            dve.sem_inc(s_store, 16)
            dve.wait_ge(s_in_mu, 32)
            nc.vector.tensor_scalar(mu[:, 2:4], mu[:, 0:2], -1.0, 1.0, ALU.mult, ALU.add).then_inc(s_mu, 1)
            nc.vector.memset(seq_sb[:, NEAR:], MASKED).then_inc(s_seq, 1)
            dve.wait_ge(s_rpe_t, 1)
            nc.vector.tensor_copy(rpe_t, ps_t[0][:, 0:2 * HEADS].rearrange("p (a n) -> p a n", a=2)).then_inc(s_rpe_t, 1)
            dve.wait_ge(s_seq_mm, 1)
            nc.vector.tensor_copy(seq_sb[:, 0:NEAR], ps_t[1][0:HEADS, 0:NEAR]).then_inc(s_seq, 1)
            dve.wait_ge(s_wt, 1)
            nc.vector.tensor_copy(w_t[:, :, :], ps_o[:, 0:3 * P].rearrange("p (a n) -> p a n", a=3)).then_inc(s_wt, 1)

            def project(m, c):
                dve.wait_ge(s_hi, 4 * m + c + 1)
                hi, lo, scale = (q_hi, q_lo, SCALE) if c < 2 else (k_hi, k_lo, 1.0)
                half = slice(512 * (c % 2), 512 * (c % 2) + 512)
                nc.vector.scalar_tensor_tensor(out=lo[:, half], in0=ps_m[:, :], scalar=scale,
                                               in1=hi[:, half].bitcast(F32), op0=ALU.mult, op1=ALU.subtract)\
                    .then_inc(s_lo, 1)

            def bias(n, r):
                h, i = ROWS[r]
                width = P * (i + 1)
                if i % GROUP == 0:
                    dve.wait_ge(s_table[h], 16 * n + 16)
                before = (r - PSLOTS) % NROWS
                dve.wait_ge(s_tr, NBANKS * (n if before > r else n + 1) + sum(b[0] <= before for b in BANKS))
                dve.wait_ge(s_score, NROWS * n + r + 1)
                lone(dve)
                nc.vector.tensor_tensor_reduce(prob[:, r % PSLOTS, 0:width], ps_s[r % 2][:, 0:width],
                                               table[:, h, SEQ - width:], 1.0, 3.0e38, ALU.add, ALU.min,
                                               low[:, r:r + 1]).then_inc(s_biased, 1)

            def invert(n, r):
                dve.wait_ge(s_exp, NROWS * n + r + 1)
                nc.vector.reciprocal(inv[:, r:r + 1], total[:, r:r + 1]).then_inc(s_inv, 1)

            def evacuate(n, k):
                r, b0, nb = BANKS[k]
                h, i = ROWS[r]
                g = i // GROUP
                dve.wait_ge(s_pv, 2 * n + g + 1)
                dve.wait_ge(s_tr, NBANKS * (n + 1) + k + 1)
                nc.vector.tensor_copy(pt[h][g][:, b0:b0 + nb, P * (i % GROUP):P * (i % GROUP) + P],
                                      ps_t[0][:, 0:nb * P].rearrange("p (b s) -> p b s", s=P)).then_inc(s_ev[0], 1)

            def store_mix(n, g):
                dve.wait_ge(s_pv, 2 * n + g + 3)
                dst = mix_t[:, bass.ds(n % (2 * PAIRS), 1), GROUP * P * g:GROUP * P * (g + 1)]
                nc.vector.tensor_scalar(dst.rearrange("p a s -> p (a s)"), ps_o[:, :], 1.0, None, ALU.mult)\
                    .then_inc(s_o, 1)

            def tile_step(n, slot):
                e = n - PAIRS

                def link(ins, k):
                    ins.then_inc(s_chain, 1)
                    dve.wait_ge(s_chain, CH * (e + 1) + k)

                if slot == EP1:
                    dve.wait_ge(s_e1, e + 1)
                    dve.wait_ge(s_xres, 16 * e + 16)
                    link(nc.vector.tensor_tensor(y1[:, :], ps_m[:, 0:C], x_res[:, :], ALU.add), 1)
                    link(nc.vector.bn_stats(stats[:, 0, :], y1[:, :]), 2)
                    lone(dve)
                    nc.vector.bn_aggr(mv[:, 0, :], stats[:, 0, :]).then_inc(s_chain, 1)
                if slot == EP1 + 1:
                    dve.wait_ge(s_rstd, 2 * e + 1)
                    nc.vector.tensor_scalar(x1[:, :], y1[:, :], mv[:, 0, 0:1], rstd[:, 0:1],
                                            ALU.subtract, ALU.mult).then_inc(s_chain, 1)
                if slot == EP2 + 1:
                    dve.wait_ge(s_x1t, e + 1)
                    for a, dst in enumerate((xr_t, xk_t)):
                        ins = nc.vector.tensor_scalar(shift[:, a, :], x1_t[:, bass.ds(n % TILES * P, P)],
                                                      mu[:, 2 + a:3 + a], None, ALU.mult)
                        if a == 1:
                            link(ins, 5)
                    for a, dst in enumerate((xr_t, xk_t)):
                        ins = nc.vector.scalar_tensor_tensor(out=dst[:, :], in0=x1_t[:, bass.ds(1 + n % TILES * P, P)],
                                                             scalar=mu[:, a:a + 1], in1=shift[:, a, :],
                                                             op0=ALU.mult, op1=ALU.add)
                    ins.then_inc(s_chain, 1)
                if slot == EP3 + 1:
                    dve.wait_ge(s_sig, e + 1)
                    nc.vector.tensor_tensor(k_act[:, :], k_act[:, :], k_act[:, :], ALU.mult)
                    link(nc.vector.tensor_scalar(gate1[:, :], gate, 1.0, None, ALU.add), 7)
                if slot == EP4:
                    link(nc.vector.reciprocal(gate, gate1[:, :]), 8)
                    dve.wait_ge(s_e8, e + 1)
                    link(nc.vector.tensor_tensor(y2[:, :], ps_m[:, 0:C], gate, ALU.mult), 9)
                    link(nc.vector.tensor_tensor(y3, y2[:, :], x1[:, :], ALU.add), 10)
                    link(nc.vector.bn_stats(stats[:, 1, :], y3), 11)
                    lone(dve)
                    nc.vector.bn_aggr(mv[:, 1, :], stats[:, 1, :]).then_inc(s_chain, 1)
                if slot == EP4 + 1:
                    dve.wait_ge(s_rstd, 2 * e + 2)
                    nc.vector.tensor_scalar(o_tile[:, :], y3, mv[:, 1, 0:1], rstd[:, 1:2],
                                            ALU.subtract, ALU.mult).then_inc(s_chain, 1)

            for c in range(4):
                project(0, c)

            def step(n, tile_too, more):
                for r in range(LEAD):
                    bias(n, r)
                    if r:
                        invert(n, r - 1)
                for slot in range(NROWS):
                    if more and 0 <= slot - PROJ_SLOT < 4:
                        project(n + 1, slot - PROJ_SLOT)
                    if slot + LEAD < NROWS:
                        bias(n, slot + LEAD)
                    if slot + LEAD - 1 < NROWS:
                        invert(n, slot + LEAD - 1)
                    if slot == 2 * GROUP + 1:
                        store_mix(n, 0)
                    for k in range(0, NBANKS, 2):
                        if BANKS[k][0] == slot:
                            evacuate(n, k)
                    if tile_too:
                        tile_step(n, slot)
                store_mix(n, 1)

            def tile(n):
                for slot in range(NROWS):
                    tile_step(n, slot)

            drive(dve, step, tile)

        @block.tensor
        def _(pe):
            pe.wait_ge(s_const, 2)
            pe.wait_ge(s_in_rpe, 16)
            for a in range(2):
                ins = nc.tensor.transpose(ps_t[0][:, HEADS * a:HEADS * a + HEADS],
                                          pt[0][0][0:HEADS, 0, P * a:P * a + P], ident[0:HEADS, 0:HEADS])
            ins.then_inc(s_rpe_t, 1)
            for g in range(BATCH):
                pe.wait_ge(s_in_x, 16 if g == 0 else 32)
                if g >= 2:
                    pe.wait_ge(s_xt, g - 1)
                for t in range(TILES):
                    ins = nc.tensor.transpose(ps_s[g % 2][:, P * t:P * t + P], x_in[:, TILES * g + t, :], ident[:, :])
                ins.then_inc(s_setup_t, 1)
            pe.wait_ge(s_rpe_t, 2)
            pe.wait_ge(s_const, 4)
            for a in range(2):
                ins = nc.tensor.matmul(ps_t[1][0:HEADS, :], rpe_t[:, a, :], upper[:, a, :], start=(a == 0), stop=(a == 1))
            ins.then_inc(s_seq_mm, 1)
            pe.wait_ge(s_in_w, 64)
            for a in range(3):
                ins = nc.tensor.transpose(ps_o[:, P * a:P * a + P], w_raw[:, a, :], ident[:, :])
            ins.then_inc(s_wt, 1)

            def project(m, c, tile_too):
                if c == 0:
                    pe.wait_ge(s_load, 32 * m + 32)
                    if not isinstance(m, int):
                        pe.wait_ge(s_v, 2 * m)
                        if tile_too:
                            pe.wait_ge(s_chain, CH * (m - PAIRS))
                elif c < 5:
                    pe.wait_ge(s_lo, 4 * m + c)
                else:
                    pe.wait_ge(s_v, 2 * m + 1)
                if c < 4:
                    ins = nc.tensor.matmul(ps_m[:, :], w_cur[:, c // 2, :], x_cur[:, 512 * (c % 2):512 * (c % 2) + 512],
                                           start=True, stop=True)
                else:
                    for t in range(4):
                        at = P * (4 * (c - 4) + t)
                        ins = nc.tensor.matmul(ps_m[:, P * t:P * t + P], x_cur[:, at:at + P], w_cur[:, 2, :],
                                               start=True, stop=True)
                ins.then_inc(s_proj, 1)

            def score(n, r):
                h, i = ROWS[r]
                if i % GROUP == 0:
                    pe.wait_ge(s_stack[h], 96 * n + 96)
                pe.wait_ge(s_biased, NROWS * n + r + 1)
                for c0 in range(0, P * (i + 1), 512):
                    cols = slice(c0, c0 + max(256, min(512, P * (i + 1) - c0)))
                    for k_st in (kh_st[h], kl_st[h]):
                        ins = nc.tensor.matmul(ps_s[r % 2][:, cols], q_st[h][:, P * i:P * i + P], k_st[:, cols],
                                               start=(k_st is kh_st[h]), stop=(k_st is kl_st[h]))
                ins.then_inc(s_score, 1)

            def transpose(n, r):
                pe.wait_ge(s_norm, NROWS * n + r + 1)
                for k in (k for k in range(NBANKS) if BANKS[k][0] == r):
                    _, b0, nb = BANKS[k]
                    pe.wait_ge(s_ev[k % 2], NBANKS // 2 * n + k // 2 + 1)
                    for b in range(nb):
                        at = P * (b0 + b)
                        ins = nc.tensor.transpose(ps_t[k % 2][:, P * b:P * b + P], prob[:, r % PSLOTS, at:at + P],
                                                  ident[:, :])
                    ins.then_inc(s_tr, 1)

            def mix(n, g):
                if g == 0:
                    pe.wait_ge(s_vcur, 16 * n + 16)
                for which in range(2):
                    pe.wait_ge(s_ev[which], NBANKS // 2 * n + (4 if g == 0 else 12) + 1)
                pe.wait_ge(s_o, 2 * n + g + 1)
                lone(pe)
                tiles = GROUP * (g + 1)
                for j in range(tiles):
                    c0 = P * max(0, j - GROUP * g)
                    for h in range(2):
                        ins = nc.tensor.matmul(ps_o[D * h:D * h + D, c0:], v_cur[:, j, D * h:D * h + D],
                                               pt[h][g][:, j, c0:], start=(j == 0), stop=(j == tiles - 1))
                ins.then_inc(s_pv, 1)

            def tile_step(n, slot, more=False):
                e = n - PAIRS
                if slot == EP1:
                    last_ps_m(pe, n, more)
                    pe.wait_ge(s_chain, CH * (e + 1))
                    pe.wait_ge(s_mixt, 16 * e + 16)
                    for p in range(PAIRS):
                        ins = nc.tensor.matmul(ps_m[:, 0:C], mix_tile[:, p, :], wo[:, p, :],
                                               start=(p == 0), stop=(p == PAIRS - 1))
                    ins.then_inc(s_e1, 1)
                if slot == EP2:
                    pe.wait_ge(s_chain, CH * (e + 1) + 4)
                    nc.tensor.transpose(ps_m[:, 0:P], x1[:, :], ident[:, :]).then_inc(s_e4, 1)
                if slot == EP3:
                    pe.wait_ge(s_chain, CH * (e + 1) + 6)
                    nc.tensor.matmul(ps_m[:, 0:P], xr_t[:, :], w_t[:, 0, :], start=True, stop=True)
                    nc.tensor.matmul(ps_m[:, P:2 * P], w_t[:, 1, :], xk_t[:, :], start=True, stop=True)\
                        .then_inc(s_e6, 1)
                if slot == EP4:
                    pe.wait_ge(s_chain, CH * (e + 1) + 7)
                    nc.tensor.matmul(ps_m[:, 0:C], k_act[:, :], w_t[:, 2, :], start=True, stop=True).then_inc(s_e8, 1)

            pe.sem_inc(s_tr, NBANKS)
            pe.sem_inc(s_pv, 2)
            pe.wait_ge(s_wt, 2)
            for c in range(NPROJ):
                project(0, c, False)

            def step(n, tile_too, more):
                for r in range(LEAD):
                    score(n, r)
                for slot in range(NROWS):
                    if more and 0 <= slot - PROJ_SLOT < NPROJ:
                        project(n + 1, slot - PROJ_SLOT, tile_too)
                    if tile_too:
                        tile_step(n, slot, more)
                    if slot + LEAD < NROWS:
                        score(n, slot + LEAD)
                    if slot == 2 * GROUP:
                        mix(n, 0)
                    transpose(n, slot)
                mix(n, 1)

            def tile(n):
                for slot in range(NROWS):
                    tile_step(n, slot)

            drive(pe, step, tile)


_INS = ['L0_attn_x', 'L0_attn_qkv', 'L0_attn_out_w', 'L0_attn_rpe_bias', 'L0_ffn_W_r', 'L0_ffn_W_k', 'L0_ffn_W_v',
        'L0_ffn_mu_r', 'L0_ffn_mu_k']


def kernel(**inputs):
    import numpy as _np
    import concourse.bacc as _bacc
    from concourse import mybir as _mybir
    from concourse.bass_utils import run_bass_kernel_spmd as _run

    nc = _bacc.Bacc("TRN2", target_bir_lowering=False, num_devices=1)
    arrays, args = {}, []
    for name in _INS:
        a = _np.ascontiguousarray(inputs[name])
        arrays[f"in_{name}"] = a
        args.append(nc.dram_tensor(f"in_{name}", a.shape, _mybir.dt.from_np(a.dtype), kind="ExternalInput").ap())
    shape = inputs['L0_attn_x'].shape
    args.append(nc.dram_tensor("out_y", shape, _mybir.dt.float32, kind="ExternalOutput").ap())
    build(nc, *args)
    r = _run(nc, [arrays], core_ids=[0])
    return r.results[0]["out_y"]
```

```python
import concourse.bass as bass
from concourse import mybir
from contextlib import ExitStack

F32 = mybir.dt.float32
F32R = mybir.dt.float32r
ALU = mybir.AluOpType
ACT = mybir.ActivationFunctionType

BATCH, SEQ, C = 4, 1024, 128
HEADS, D, SPAN = 16, 64, 256
P = 128
PAIRS = HEADS // 2
PAIR_STEPS = BATCH * PAIRS
TILES = SEQ // P
GROUP = 4
NEAR = SPAN + P
FAR = SEQ - NEAR
MASKED = 30000.0
EPS = 1e-5
SCALE = -(D ** -0.5)

ROWS = [(h, i) for g in range(TILES // GROUP) for h in range(2) for i in range(GROUP * g, GROUP * g + GROUP)]
NROWS = len(ROWS)
LEAD = 4
PSLOTS = 8


def bank_list():
    out = []
    for r, (_, i) in enumerate(ROWS):
        for b0 in range(0, i + 1, 4):
            out.append((r, b0, min(4, i + 1 - b0)))
    return out


def score_at(r):
    return SEQ // 2 * (r % 4) if r < NROWS // 2 else SEQ * (r % 2)


def score_end(r):
    return score_at(r) + P * (ROWS[r][1] + 1 if ROWS[r][1] >= GROUP else GROUP)


def rows_since(r):
    return next(k for k in range(1, NROWS)
                if score_at((r - k) % NROWS) < score_end(r) and score_at(r) < score_end((r - k) % NROWS))


BANKS = bank_list()
NBANKS = len(BANKS)
PROJ_SLOTS = (2, 3, 5, 7, 10, 14)
NPROJ = len(PROJ_SLOTS)
OUT_PROJ, LN1_RSTD, LN1 = 0, 0, 1
X1_T, SHIFT = 4, 4
RK_PROJ, GATE = 8, 9
V_PROJ, LN2_RSTD, LN2 = 12, 13, 14
TILE_MATMULS = (OUT_PROJ, X1_T, RK_PROJ, V_PROJ)
WIDE = 4
ACT_ORDER, DVE_ORDER, PE_ORDER = 'pexv', 'bipvfe', 'spefmt'
MIX_FAR = 0
MIX_NEAR = 11
TILE_LAG = PAIRS + 1
CH = 13


def build(nc, x, qkv, out_w, rpe, w_r, w_k, w_v, mu_r, mu_k, out):
    seq_d = nc.dram_tensor("bias_by_distance", (HEADS, P, 4 * P), F32, kind="Internal").ap()
    toeplitz = bass.AP(seq_d.tensor, P - 1, [[P * 4 * P, HEADS], [4 * P - 1, P], [1, NEAR]])
    mix_d = nc.dram_tensor("mix_transposed", (PAIR_STEPS, P, SEQ), F32, kind="Internal").ap()
    xt_d = nc.dram_tensor("x_transposed", (BATCH, P, SEQ), F32, kind="Internal").ap()

    x_tiles = x.rearrange("b (t p) c -> p (b t) c", p=P)
    x_rows = x.rearrange("b s c -> (b s) c")
    out_rows = out.rearrange("b s c -> (b s) c")
    qkv_pairs = qkv.rearrange("c m (r h) d -> r c m (h d)", h=2)
    wo_pairs = out_w.rearrange("(r h) d c -> (h d) r c", h=2)

    with ExitStack() as ctx:
        def sb(name, shape, dt=F32):
            return ctx.enter_context(nc.sbuf_tensor(name, shape, dt))

        def ps(name, shape):
            return ctx.enter_context(nc.psum_tensor(name, shape, F32))

        def sem(name):
            return ctx.enter_context(nc.semaphore(name))

        ident = sb("ident", [P, P])
        wo = sb("wo", [P, PAIRS, C])
        w_t = sb("w_t", [P, 3, C])
        mu = sb("mu", [P, 4])
        eps = sb("eps", [P, 1])
        x_cur = sb("x_cur", [P, SEQ])
        w_cur = sb("w_cur", [P, 3, P])
        q_hi, q_lo, k_hi, k_lo = (sb(n, [P, SEQ], F32R) for n in ("q_hi", "q_lo", "k_hi", "k_lo"))
        v_new = sb("v_new", [P, 2, TILES, P])
        q_st = [sb(f"q_st{h}", [P, SEQ], F32R) for h in range(2)]
        kh_st = [sb(f"kh_st{h}", [P, SEQ], F32R) for h in range(2)]
        kl_st = [sb(f"kl_st{h}", [P, SEQ], F32R) for h in range(2)]
        v_cur = sb("v_cur", [P, TILES, P])
        table = sb("table", [P, 2, SEQ])
        prob = sb("prob", [P, PSLOTS, SEQ])
        low = sb("low", [P, NROWS])
        total = sb("total", [P, NROWS])
        inv = sb("inv", [P, NROWS])
        pt = [[sb(f"pt{h}{g}", [P, GROUP * (g + 1), GROUP * P]) for g in range(2)] for h in range(2)]
        mix_sb = [sb(f"mix_sb{g}", [P, GROUP * P]) for g in range(2)]
        mix_tile = sb("mix_tile", [P, PAIRS, P])
        x_res = sb("x_res", [P, C])
        y1 = sb("y1", [P, C])
        o_tile = sb("o_tile", [P, C])
        x1 = sb("x1", [P, C])
        x1_t = sb("x1_t", [P, 1 + SEQ])
        shift = sb("shift", [P, 2, P])
        xr_t = sb("xr_t", [P, P])
        xk_t = sb("xk_t", [P, P])
        gate1, k_act, y2 = xr_t, xk_t, y1
        y3, gate = shift[:, 0, :], shift[:, 1, :]
        stats = sb("stats", [P, 2, 6])
        mv = sb("mv", [P, 2, 2])
        lnv = sb("lnv", [P, 2])
        rstd = sb("rstd", [P, 2])

        mix_last = sb("mix_last", [P, PAIRS - 1, SEQ])
        x_last = x_cur[:, :].rearrange("p (t c) -> p t c", c=C)
        y1_l, x1_l, shr_l, shk_l, xr_l, xk_l, gate_l, k_l = (prob[:, k, :] for k in range(8))
        y3_l, o_l = shr_l, shk_l
        stats_l = sb("stats_last", [P, 2, TILES, 6])
        mv_l = sb("mv_last", [P, 2, TILES, 2])
        lnv_l = sb("lnv_last", [P, 2, TILES])
        rstd_l = sb("rstd_last", [P, 2, TILES])

        x_t = mix_last[:, 0:BATCH, :].rearrange("p b s -> p (b s)")
        x_in = prob[:, 0:BATCH, :].rearrange("p a (t c) -> p (a t) c", c=C)
        rpe_in = pt[0][0][0:HEADS, 0, 0:SPAN]
        rpe_t = pt[0][0][:, 1, 0:2 * HEADS].rearrange("p (a n) -> p a n", a=2)
        upper = pt[1][0][:, 0:2, :]
        w_raw = pt[1][1][:, 0, 0:3 * C].rearrange("p (a c) -> p a c", a=3)
        seq_sb = x1_t[0:HEADS, 1:1 + 4 * P]

        ps_rows = ps("ps_rows", [P, 2 * SEQ])
        ps_s = [ps_rows[:, SEQ * k:SEQ * k + SEQ] for k in range(2)]
        ps_t = [ps(f"ps_t{k}", [P, 4 * P]) for k in range(2)]
        ps_o = ps("ps_o", [P, GROUP * P])
        ps_m = ps("ps_m", [P, 4 * P])

        s_in_x, s_in_w, s_in_rpe, s_in_mu = sem("in_x"), sem("in_w"), sem("in_rpe"), sem("in_mu")
        s_const = sem("const")
        s_zero = sem("zero")
        s_setup_t = sem("setup_transposed")
        s_xt = sem("xt_copied")
        s_wt = sem("wt_copied")
        s_rpe_t = sem("rpe_t")
        s_seq_mm = sem("seq_matmul")
        s_seq = sem("seq_ready")
        s_seq_dram = sem("seq_in_dram")
        s_xt_dram = sem("xt_in_dram")
        s_mu = sem("mu_ready")
        s_load = sem("pair_loaded")
        s_proj = sem("projected")
        s_hi = sem("hi_ready")
        s_lo = sem("lo_ready")
        s_v = sem("v_ready")
        s_first = [sem(f"first_half{h}") for h in range(2)]
        s_stack = [sem(f"stacked{h}") for h in range(2)]
        s_table = [sem(f"table{h}") for h in range(2)]
        s_vcur = sem("v_cur_loaded")
        s_score = sem("scored")
        s_biased = sem("biased")
        s_exp = sem("exped")
        s_inv = sem("inverted")
        s_norm = sem("normalised")
        s_tr = sem("transposed")
        s_ev = [sem("evacuated_dve"), sem("evacuated_act")]
        s_pv = sem("mixed")
        s_o = sem("mix_evacuated")
        s_mix_d = [sem(f"mix_in_dram{g}") for g in range(2)]
        s_xres, s_mixt = sem("x_res_loaded"), sem("mix_tile_loaded")
        s_e1, s_e4, s_e6, s_e8 = sem("out_projected"), sem("x1_transposed"), sem("rk_projected"), sem("v_projected")
        s_chain = sem("tile_chain")
        s_ln = sem("log_var")
        s_rstd = sem("rstd_ready")
        s_x1t = sem("x1_t_ready")
        s_sig = sem("exp_gate")
        s_store = sem("stored")
        s_own = sem("own_instruction")
        last = {k: sem(f"last_{k}") for k in (
            "x_loaded", "mix_loaded", "out_projected", "pair_projected", "part1", "y1", "stats1", "mv1", "ln1", "rstd1", "x1",
            "x1_transposed", "x1_t", "shifted", "xrk", "rk_projected", "exp_gate", "k_squared", "gate1", "gate",
            "v_projected", "y2", "y3", "stats2", "mv2", "ln2", "rstd2", "out", "stored")}

        def lone(e):
            e.sem_inc(s_own, 1)

        def drive(e, step, before_tiles=lambda: None):
            step(0, prev=False, tile_too=False, more=True)
            with e.Fori(1, TILE_LAG) as n:
                step(n, prev=True, tile_too=False, more=True)
            before_tiles()
            with e.Fori(TILE_LAG, PAIR_STEPS - 1) as n:
                step(n, prev=True, tile_too=True, more=True)
            step(PAIR_STEPS - 1, prev=True, tile_too=True, more=False)

        def proj_bank(m, c):
            if isinstance(m, int) and m == 0:
                return (ps_m[:, :], ps_o[:, :], ps_s[1][:, 0:512], ps_s[1][:, 512:])[c % 4]
            return ps_m[:, :]

        def rows_ahead(n, more, slot):
            if slot + LEAD < NROWS:
                return [(n, slot + LEAD)]
            return [(n + 1, slot + LEAD - NROWS)] if more else []

        block = ctx.enter_context(nc.Block())

        @block.sync
        def _(sp):
            sp.dma_start(x_in[:, 0:TILES, :], x_tiles[:, 0:TILES, :]).then_inc(s_in_x, 16)
            sp.dma_start(rpe_in, rpe).then_inc(s_in_rpe, 16)
            sp.dma_start(w_cur[:, :, :], qkv_pairs[0, :, :, :]).then_inc(s_load, 16)
            sp.dma_start(x_in[:, TILES:, :], x_tiles[:, TILES:, :]).then_inc(s_in_x, 16)
            for n, w in enumerate((w_r, w_k, w_v)):
                sp.dma_start(w_raw[:, n, :], w).then_inc(s_in_w, 16)
            sp.dma_start(wo[:, :, :], wo_pairs).then_inc(s_in_w, 16)
            for n, m in enumerate((mu_r, mu_k)):
                sp.dma_start(mu[:, n:n + 1], m.rearrange("(c a) -> c a", a=1)).then_inc(s_in_mu, 16)
            sp.wait_ge(s_seq, 2)
            copies = seq_sb.unsqueeze(1).broadcast_to([HEADS, P, 4 * P])
            sp.dma_start(seq_d[0:2, :, :], copies[0:2, :, :]).then_inc(s_seq_dram, 16)
            sp.wait_ge(s_seq_dram, 16)
            sp.wait_ge(s_zero, 1)
            for h in range(2):
                sp.dma_start(table[:, h, FAR:], toeplitz[h, :, :]).then_inc(s_table[h], 16)

            def stack(h, done, cols=slice(0, SEQ)):
                own = slice(D * h, D * h + D)
                for dst, top, bottom in ((q_st[h], q_hi, q_lo), (kh_st[h], k_hi, k_hi), (kl_st[h], k_lo, k_lo)):
                    sp.dma_start(dst[0:D, cols].bitcast(F32), top[own, cols].bitcast(F32)).then_inc(done, 16)
                    sp.dma_start(dst[D:P, cols].bitcast(F32), bottom[own, cols].bitcast(F32)).then_inc(done, 16)

            sp.wait_ge(s_lo, 4)
            for h in range(2):
                stack(h, s_first[h], slice(0, SEQ // 2))
            sp.wait_ge(s_proj, NPROJ)
            sp.sem_inc(s_load, 16)
            sp.dma_start(w_cur[:, :, :], qkv_pairs[1, :, :, :]).then_inc(s_load, 16)
            stack(0, s_stack[0], slice(SEQ // 2, SEQ))
            sp.wait_ge(s_v, 2)
            sp.dma_start(v_cur[:, :, :], v_new[:, 0, :, :]).then_inc(s_vcur, 16)
            stack(1, s_stack[1], slice(SEQ // 2, SEQ))
            sp.dma_start(seq_d[2:, :, :], copies[2:, :, :]).then_inc(s_seq_dram, 16)
            sp.wait_ge(s_xt, BATCH)
            sp.dma_start(xt_d.rearrange("b c s -> c b s"), mix_last[:, 0:BATCH, :]).then_inc(s_xt_dram, 16)
            sp.wait_ge(s_seq_dram, 32)
            sp.wait_ge(s_xt_dram, 16)

            def loads(m):
                sp.wait_ge(s_proj, NPROJ * m)
                lone(sp)
                sp.dma_start(w_cur[:, :, :], qkv_pairs[bass.ds(m % PAIRS, 1), :, :, :]).then_inc(s_load, 16)
                sp.dma_start(x_cur[:, :], xt_d[bass.ds(m // PAIRS % BATCH, 1), :, :]).then_inc(s_load, 16)

            def store_mix(n, g):
                sp.wait_ge(s_o, 2 * n + g + 2)
                lone(sp)
                sp.dma_start(mix_d[bass.ds(n, 1), :, GROUP * P * g:GROUP * P * (g + 1)], mix_sb[g][:, :])\
                    .then_inc(s_mix_d[g], 16)

            def tile_loads(n):
                sp.wait_ge(s_chain, CH * (n - TILE_LAG) + 1)
                lone(sp)
                sp.dma_start(x_res[:, :], x_rows[bass.ds((n - TILE_LAG) * P, P), :]).then_inc(s_xres, 16)
                for g in range(2):
                    sp.wait_ge(s_mix_d[g], 16 * n)
                    lone(sp)
                tiles = mix_d.rearrange("(b r) d (t s) -> b t d r s", r=PAIRS, s=P)
                e = n - TILE_LAG
                sp.dma_start(mix_tile[:, :, :], tiles[bass.ds(e // TILES, 1), bass.ds(e % TILES, 1), :, :, :])\
                    .then_inc(s_mixt, 16)

            def tile_store(n):
                sp.wait_ge(s_chain, CH * (n - TILE_LAG) + 2 * CH)
                lone(sp)
                sp.dma_start(out_rows[bass.ds((n - TILE_LAG) * P, P), :], o_tile[:, :]).then_inc(s_store, 16)

            def restack(n, h):
                rows = NROWS - GROUP * (1 - h)
                sp.wait_ge(s_score, NROWS * n + rows)
                stack(h, s_stack[h])
                sp.wait_ge(s_biased, NROWS * n + rows + 2)
                lone(sp)
                sp.dma_start(table[:, h, FAR:],
                             toeplitz[bass.ds((n + 1) % PAIRS * 2 + h, 1), :, :]).then_inc(s_table[h], 16)

            def step(n, prev, tile_too, more):
                if prev:
                    sp.wait_ge(s_v, 2 * n + 2)
                    sp.wait_ge(s_pv, 2 * n + 2)
                    lone(sp)
                    sp.dma_start(v_cur[:, :, :], v_new[:, bass.ds(n % 2, 1), :, :]).then_inc(s_vcur, 16)
                if more:
                    sp.wait_ge(s_lo, 4 * n + 8)
                    lone(sp)
                    restack(n, 0)
                if prev:
                    store_mix(n - 1, 1)
                if more:
                    restack(n, 1)
                if tile_too and more:
                    tile_loads(n + 1)
                if more:
                    loads(n + 2)
                if not more:
                    sp.wait_ge(s_proj, NPROJ * PAIR_STEPS)
                    sp.wait_ge(s_load, 32 * (PAIR_STEPS + 1))
                    sp.dma_start(x_last, x_tiles[:, TILES * (BATCH - 1):, :]).then_inc(last["x_loaded"], 16)
                    for g in range(2):
                        sp.wait_ge(s_mix_d[g], 16 * PAIR_STEPS)
                    sp.dma_start(mix_last[:, :, :], mix_d[PAIR_STEPS - PAIRS:PAIR_STEPS - 1, :, :]
                                 .rearrange("r d s -> d r s")).then_inc(last["mix_loaded"], 16)
                if tile_too:
                    tile_store(n)
                if more:
                    store_mix(n, 0)

            drive(sp, step, before_tiles=lambda: tile_loads(TILE_LAG))
            tile_loads(PAIR_STEPS)
            tile_store(PAIR_STEPS)
            for w in range(TILES // WIDE):
                sp.wait_ge(last["out"], w + 1)
                sp.dma_start(out.rearrange("b (t p) c -> b p t c", p=P)[BATCH - 1, :, WIDE * w:WIDE * (w + 1), :],
                             o_l[:, WIDE * P * w:WIDE * P * (w + 1)].rearrange("p (t c) -> p t c", c=C))\
                    .then_inc(last["stored"], 16)
            sp.wait_ge(last["stored"], 16 * TILES // WIDE)
            sp.wait_ge(s_store, 16 * (BATCH - 1) * TILES + 16)

        @block.gpsimd
        def _(pool):
            pool.memset(ident[:, :], 0.0).then_inc(s_const, 1)
            pool.wait_ge(s_const, 1)
            pool.affine_select(out=ident[:, :], in_=ident[:, :], compare_op=ALU.not_equal, fill=1.0, base=0,
                               pattern=[[-1, P]], channel_multiplier=1).then_inc(s_const, 1)
            pool.memset(upper, 1.0).then_inc(s_const, 1)
            pool.wait_ge(s_const, 3)
            pool.affine_select(out=upper, in_=upper, compare_op=ALU.is_gt, fill=0.0, base=-(NEAR - 1),
                               pattern=[[P, 2], [1, 4 * P]], channel_multiplier=1).then_inc(s_const, 1)
            pool.memset(table[:, :, 0:FAR], 0.0).then_inc(s_zero, 1)
            pool.memset(x1_t[:, 0:1], 0.0).then_inc(s_zero, 1)
            pool.memset(eps[:, :], EPS).then_inc(s_zero, 1)

            def normalise(n, r):
                width = P * (ROWS[r][1] + 1)
                pool.wait_ge(s_inv, NROWS * n + r + 1)
                row = prob[:, r % PSLOTS, 0:width]
                nc.gpsimd.tensor_tensor(row, row, inv[:, r:r + 1].broadcast_to([P, width]), ALU.mult)\
                    .then_inc(s_norm, 1)

            with pool.Fori(0, PAIR_STEPS) as n:
                for r in range(NROWS):
                    normalise(n, r)
            for w in range(TILES // WIDE):
                cols = slice(WIDE * P * w, WIDE * P * (w + 1))
                pool.wait_ge(last["exp_gate"], w + 1)
                nc.gpsimd.tensor_tensor(k_l[:, cols], k_l[:, cols], k_l[:, cols], ALU.mult)\
                    .then_inc(last["k_squared"], 1)

        @block.scalar
        def _(act):
            nc.scalar.preload_act_table_set("natural_log_exp_and_others")
            def copy_x(b):
                act.wait_ge(s_setup_t, b + 1)
                if b == 0:
                    act.wait_ge(s_load, 32)
                nc.scalar.activation(x_t[:, SEQ * b:SEQ * b + SEQ], ps_s[0], ACT.Copy).then_inc(s_xt, 1)

            def project(m, c):
                if c == 0 and not (isinstance(m, int) and m == 0):
                    for h in range(2):
                        if isinstance(m, int):
                            act.wait_ge(s_first[h], 96)
                        act.wait_ge(s_stack[h], 96 * m)
                act.wait_ge(s_proj, NPROJ * m + c + 1)
                if c < 4:
                    dst, scale = (q_hi, SCALE) if c < 2 else (k_hi, 1.0)
                    half = slice(512 * (c % 2), 512 * (c % 2) + 512)
                    nc.scalar.activation(dst[:, half], proj_bank(m, c), ACT.Copy, scale=scale).then_inc(s_hi, 1)
                else:
                    half = slice(4 * (c - 4), 4 * (c - 4) + 4)
                    if c == 4 and not (isinstance(m, int) and m < 2):
                        act.wait_ge(s_vcur, 16 * m - 16)
                    lone(act)
                    nc.scalar.activation(v_new[:, bass.ds(m % 2, 1), half, :], proj_bank(m, c).rearrange("p (a t d) -> p a t d", a=1, d=P),
                                         ACT.Copy).then_inc(s_v, 1)

            def exps(n, r):
                width = P * (ROWS[r][1] + 1)
                act.wait_ge(s_biased, NROWS * n + r + 3)
                row = prob[:, r % PSLOTS, 0:width]
                nc.scalar.activation(row, row, ACT.Exp, bias=low[:, r:r + 1], scale=-1.0,
                                     accum_out=total[:, r:r + 1]).then_inc(s_exp, 1)

            def evacuate(n, k):
                r, b0, nb = BANKS[k]
                h, i = ROWS[r]
                g = i // GROUP
                act.wait_ge(s_pv, 2 * n + g + 1)
                act.wait_ge(s_tr, NBANKS * (n + 1) + k + 1)
                nc.scalar.activation(pt[h][g][:, b0:b0 + nb, P * (i % GROUP):P * (i % GROUP) + P],
                                     ps_t[1][:, 0:nb * P].rearrange("p (b s) -> p b s", s=P),
                                     ACT.Copy).then_inc(s_ev[1], 1)

            def tile_step(n, slot):
                e = n - TILE_LAG
                for which, at in ((0, LN1_RSTD), (1, LN2_RSTD)):
                    if slot == at:
                        act.wait_ge(s_chain, CH * (e + 1) + (3 if which == 0 else 12))
                        nc.scalar.activation(lnv[:, which:which + 1], mv[:, which, 1:2], ACT.Ln,
                                             bias=eps[:, 0:1]).then_inc(s_ln, 1)
                        act.wait_ge(s_ln, 2 * e + which + 1)
                        nc.scalar.activation(rstd[:, which:which + 1], lnv[:, which:which + 1], ACT.Exp,
                                             scale=-0.5).then_inc(s_rstd, 1)
                if slot == X1_T:
                    act.wait_ge(s_e4, e + 1)
                    lone(act)
                    nc.scalar.activation(x1_t[:, bass.ds(1 + (n - TILE_LAG) % TILES * P, P)], ps_m[:, 0:P], ACT.Copy)\
                        .then_inc(s_x1t, 1)
                if slot == RK_PROJ:
                    act.wait_ge(s_e6, e + 1)
                    nc.scalar.activation(gate, ps_m[:, 0:P], ACT.Exp, scale=-1.0)
                    nc.scalar.activation(k_act[:, :], ps_m[:, P:2 * P], ACT.Relu).then_inc(s_sig, 1)

            copy_x(0)
            for c in range(NPROJ):
                project(0, c)
                if c % 2:
                    copy_x(1 + c // 2)
            act.wait_ge(s_zero, 3)

            for r in range(LEAD):
                exps(0, r)

            def step(n, prev, tile_too, more):
                for slot in range(NROWS):
                  for o in ACT_ORDER:
                    if o == 'p' and more and slot in PROJ_SLOTS:
                        project(n + 1, PROJ_SLOTS.index(slot))
                    if o == 'x':
                      for row in rows_ahead(n, more, slot):
                        exps(*row)
                    if o == 'v':
                      for k in range(1, NBANKS, 2):
                        if BANKS[k][0] == slot:
                            evacuate(n, k)
                    if o == 'e' and tile_too:
                        tile_step(n, slot)

            drive(act, step)
            for slot in range(NROWS):
                tile_step(PAIR_STEPS, slot)

            def ln_rstd(which, w):
                tiles = slice(WIDE * w, WIDE * (w + 1))
                act.wait_ge(last[f"mv{which + 1}"], w + 1)
                nc.scalar.activation(lnv_l[:, which, tiles], mv_l[:, which, tiles, 1], ACT.Ln, bias=eps[:, 0:1])\
                    .then_inc(last[f"ln{which + 1}"], 1)
                act.wait_ge(last[f"ln{which + 1}"], w + 1)
                nc.scalar.activation(rstd_l[:, which, tiles], lnv_l[:, which, tiles], ACT.Exp, scale=-0.5)\
                    .then_inc(last[f"rstd{which + 1}"], 1)

            groups = [(w, slice(WIDE * P * w, WIDE * P * (w + 1))) for w in range(TILES // WIDE)]
            for w, cols in groups:
                ln_rstd(0, w)
            act.wait_ge(s_chain, CH * ((BATCH - 1) * TILES) + 6)
            for w, cols in groups:
                act.wait_ge(last["x1_transposed"], w + 1)
                nc.scalar.activation(x1_t[:, 1 + cols.start:1 + cols.stop], ps_s[1][:, cols], ACT.Copy)\
                    .then_inc(last["x1_t"], 1)
            for w, cols in groups:
                act.wait_ge(last["rk_projected"], w + 1)
                nc.scalar.activation(gate_l[:, cols], ps_s[0][:, cols], ACT.Exp, scale=-1.0)
                nc.scalar.activation(k_l[:, cols], ps_t[w][:, :], ACT.Relu).then_inc(last["exp_gate"], 1)
            for w, cols in groups:
                ln_rstd(1, w)

        @block.vector
        def _(dve):
            dve.sem_inc(s_biased, 2)
            dve.sem_inc(s_ev[0], 1)
            dve.sem_inc(s_ev[1], 1)
            dve.sem_inc(s_o, 1)
            dve.sem_inc(s_chain, CH)
            dve.sem_inc(s_store, 16)
            dve.sem_inc(s_mix_d[0], 16)
            dve.sem_inc(s_mix_d[1], 16)
            nc.vector.memset(seq_sb[:, NEAR:], MASKED).then_inc(s_seq, 1)
            dve.wait_ge(s_setup_t, 1)
            for half in (slice(0, SEQ // 2), slice(SEQ // 2, SEQ)):
                nc.vector.tensor_copy(x_cur[:, half], ps_s[0][:, half]).then_inc(s_load, 8)
            dve.wait_ge(s_rpe_t, 1)
            nc.vector.tensor_copy(rpe_t, ps_t[0][:, 0:2 * HEADS].rearrange("p (a n) -> p a n", a=2)).then_inc(s_rpe_t, 1)
            dve.wait_ge(s_seq_mm, 1)
            nc.vector.tensor_copy(seq_sb[:, 0:NEAR], ps_t[1][0:HEADS, 0:NEAR]).then_inc(s_seq, 1)

            def project(m, c):
                dve.wait_ge(s_hi, 4 * m + c + 1)
                hi, lo, scale = (q_hi, q_lo, SCALE) if c < 2 else (k_hi, k_lo, 1.0)
                half = slice(512 * (c % 2), 512 * (c % 2) + 512)
                nc.vector.scalar_tensor_tensor(out=lo[:, half], in0=proj_bank(m, c), scalar=scale,
                                               in1=hi[:, half].bitcast(F32), op0=ALU.mult, op1=ALU.subtract)\
                    .then_inc(s_lo, 1)

            def bias(n, r):
                h, i = ROWS[r]
                width = P * (i + 1)
                if i % GROUP == 0:
                    dve.wait_ge(s_table[h], 16 * n + 16)
                before = (r - PSLOTS) % NROWS
                dve.wait_ge(s_tr, NBANKS * (n if before > r else n + 1) + sum(b[0] <= before for b in BANKS))
                dve.wait_ge(s_score, NROWS * n + r + 1)
                lone(dve)
                nc.vector.tensor_tensor_reduce(prob[:, r % PSLOTS, 0:width], ps_rows[:, score_at(r):score_at(r) + width],
                                               table[:, h, SEQ - width:], 1.0, 3.0e38, ALU.add, ALU.min,
                                               low[:, r:r + 1]).then_inc(s_biased, 1)

            def invert(n, r):
                dve.wait_ge(s_exp, NROWS * n + r + 1)
                nc.vector.reciprocal(inv[:, r:r + 1], total[:, r:r + 1]).then_inc(s_inv, 1)

            def evacuate(n, k):
                r, b0, nb = BANKS[k]
                h, i = ROWS[r]
                g = i // GROUP
                dve.wait_ge(s_pv, 2 * n + g + 1)
                dve.wait_ge(s_tr, NBANKS * (n + 1) + k + 1)
                nc.vector.tensor_copy(pt[h][g][:, b0:b0 + nb, P * (i % GROUP):P * (i % GROUP) + P],
                                      ps_t[0][:, 0:nb * P].rearrange("p (b s) -> p b s", s=P)).then_inc(s_ev[0], 1)

            def store_mix(n, g):
                dve.wait_ge(s_pv, 2 * n + g + 3)
                dve.wait_ge(s_mix_d[g], 16 * n + 16)
                nc.vector.tensor_copy(mix_sb[g][:, :], ps_o[:, :]).then_inc(s_o, 1)

            def tile_step(n, slot):
                e = n - TILE_LAG

                def link(ins, k):
                    ins.then_inc(s_chain, 1)
                    dve.wait_ge(s_chain, CH * (e + 1) + k)

                if slot == OUT_PROJ:
                    dve.wait_ge(s_e1, e + 1)
                    dve.wait_ge(s_xres, 16 * e + 16)
                    link(nc.vector.tensor_tensor(y1[:, :], ps_m[:, 0:C], x_res[:, :], ALU.add), 1)
                    link(nc.vector.bn_stats(stats[:, 0, :], y1[:, :]), 2)
                    lone(dve)
                    nc.vector.bn_aggr(mv[:, 0, :], stats[:, 0, :]).then_inc(s_chain, 1)
                if slot == LN1:
                    dve.wait_ge(s_rstd, 2 * e + 1)
                    nc.vector.tensor_scalar(x1[:, :], y1[:, :], mv[:, 0, 0:1], rstd[:, 0:1],
                                            ALU.subtract, ALU.mult).then_inc(s_chain, 1)
                if slot == SHIFT:
                    dve.wait_ge(s_x1t, e + 1)
                    for a, dst in enumerate((xr_t, xk_t)):
                        ins = nc.vector.tensor_scalar(shift[:, a, :], x1_t[:, bass.ds((n - TILE_LAG) % TILES * P, P)],
                                                      mu[:, 2 + a:3 + a], None, ALU.mult)
                        if a == 1:
                            link(ins, 5)
                    for a, dst in enumerate((xr_t, xk_t)):
                        ins = nc.vector.scalar_tensor_tensor(out=dst[:, :], in0=x1_t[:, bass.ds(1 + (n - TILE_LAG) % TILES * P, P)],
                                                             scalar=mu[:, a:a + 1], in1=shift[:, a, :],
                                                             op0=ALU.mult, op1=ALU.add)
                    ins.then_inc(s_chain, 1)
                if slot == RK_PROJ:
                    dve.wait_ge(s_sig, e + 1)
                    nc.vector.tensor_tensor(k_act[:, :], k_act[:, :], k_act[:, :], ALU.mult)
                    nc.vector.tensor_scalar(gate1[:, :], gate, 1.0, None, ALU.add).then_inc(s_chain, 1)
                if slot == GATE:
                    dve.wait_ge(s_chain, CH * (e + 1) + 7)
                    nc.vector.reciprocal(gate, gate1[:, :]).then_inc(s_chain, 1)
                if slot == V_PROJ:
                    dve.wait_ge(s_e8, e + 1)
                    dve.wait_ge(s_chain, CH * (e + 1) + 8)
                    link(nc.vector.tensor_tensor(y2[:, :], ps_m[:, 0:C], gate, ALU.mult), 9)
                    link(nc.vector.tensor_tensor(y3, y2[:, :], x1[:, :], ALU.add), 10)
                    link(nc.vector.bn_stats(stats[:, 1, :], y3), 11)
                    lone(dve)
                    nc.vector.bn_aggr(mv[:, 1, :], stats[:, 1, :]).then_inc(s_chain, 1)
                if slot == LN2:
                    dve.wait_ge(s_rstd, 2 * e + 2)
                    dve.wait_ge(s_store, 16 * e + 16)
                    nc.vector.tensor_scalar(o_tile[:, :], y3, mv[:, 1, 0:1], rstd[:, 1:2],
                                            ALU.subtract, ALU.mult).then_inc(s_chain, 1)

            for c in range(4):
                project(0, c)
            dve.wait_ge(s_in_mu, 32)
            nc.vector.tensor_scalar(mu[:, 2:4], mu[:, 0:2], -1.0, 1.0, ALU.mult, ALU.add).then_inc(s_mu, 1)
            dve.wait_ge(s_wt, 1)
            nc.vector.tensor_copy(w_t[:, :, :], ps_t[0][:, 0:3 * P].rearrange("p (a n) -> p a n", a=3)).then_inc(s_wt, 1)

            for r in range(LEAD):
                bias(0, r)
                if r:
                    invert(0, r - 1)

            def step(n, prev, tile_too, more):
                for slot in range(NROWS):
                  for o in DVE_ORDER:
                    if o == 'p' and more and slot in PROJ_SLOTS[:4]:
                        project(n + 1, PROJ_SLOTS.index(slot))
                    if o == 'b':
                      for row in rows_ahead(n, more, slot):
                        bias(*row)
                    if o == 'i':
                      for row in rows_ahead(n, more, slot - 1):
                        invert(*row)
                    if o == 'f' and prev and slot == MIX_FAR + TILES:
                        store_mix(n - 1, 1)
                    if o == 'f' and slot == MIX_NEAR + GROUP:
                        store_mix(n, 0)
                    if o == 'v':
                      for k in range(0, NBANKS, 2):
                        if BANKS[k][0] == slot:
                            evacuate(n, k)
                    if o == 'e' and tile_too:
                        tile_step(n, slot)

            drive(dve, step)
            for slot in range(NROWS):
                if slot == SHIFT:
                    store_mix(PAIR_STEPS - 1, 1)
                tile_step(PAIR_STEPS, slot)

            def each(w):
                return range(WIDE * w, WIDE * (w + 1))

            def norm_stats(which, w, y):
                for t in each(w):
                    ins = nc.vector.bn_stats(stats_l[:, which, t, :], y[:, P * t:P * t + P])
                ins.then_inc(last[f"stats{which + 1}"], 1)
                dve.wait_ge(last[f"stats{which + 1}"], w + 1)
                lone(dve)
                for t in each(w):
                    ins = nc.vector.bn_aggr(mv_l[:, which, t, :], stats_l[:, which, t, :])
                ins.then_inc(last[f"mv{which + 1}"], 1)

            def normed(which, w, y, dst, done):
                dve.wait_ge(last[f"rstd{which + 1}"], w + 1)
                for t in each(w):
                    ins = nc.vector.tensor_scalar(dst[:, P * t:P * t + P], y[:, P * t:P * t + P],
                                                  mv_l[:, which, t, 0:1], rstd_l[:, which, t:t + 1],
                                                  ALU.subtract, ALU.mult)
                ins.then_inc(done, 1)

            groups = [(w, slice(WIDE * P * w, WIDE * P * (w + 1))) for w in range(TILES // WIDE)]
            dve.wait_ge(s_tr, NBANKS * (PAIR_STEPS + 1))
            dve.wait_ge(last["x_loaded"], 16)
            for w, cols in groups:
                dve.wait_ge(last["out_projected"], w + 1)
                nc.vector.tensor_tensor(y1_l[:, cols], ps_s[0][:, cols], x_cur[:, cols], ALU.add)\
                    .then_inc(last["part1"], 1)
            for w, cols in groups:
                dve.wait_ge(last["pair_projected"], w + 1)
                dve.wait_ge(last["part1"], w + 1)
                nc.vector.tensor_tensor(y1_l[:, cols], ps_s[1][:, cols], y1_l[:, cols], ALU.add)\
                    .then_inc(last["y1"], 1)
                dve.wait_ge(last["y1"], w + 1)
                norm_stats(0, w, y1_l)
            for w, cols in groups:
                normed(0, w, y1_l, x1_l, last["x1"])
            for w, cols in groups:
                dve.wait_ge(last["x1_t"], w + 1)
                for a, dst in enumerate((shr_l, shk_l)):
                    ins = nc.vector.tensor_scalar(dst[:, cols], x1_t[:, cols], mu[:, 2 + a:3 + a], None, ALU.mult)
                ins.then_inc(last["shifted"], 1)
                dve.wait_ge(last["shifted"], w + 1)
                for a, (dst, shifted) in enumerate(((xr_l, shr_l), (xk_l, shk_l))):
                    ins = nc.vector.scalar_tensor_tensor(out=dst[:, cols], in0=x1_t[:, 1 + cols.start:1 + cols.stop],
                                                         scalar=mu[:, a:a + 1], in1=shifted[:, cols],
                                                         op0=ALU.mult, op1=ALU.add)
                ins.then_inc(last["xrk"], 1)
            for w, cols in groups:
                dve.wait_ge(last["exp_gate"], w + 1)
                nc.vector.tensor_scalar(gate_l[:, cols], gate_l[:, cols], 1.0, None, ALU.add)\
                    .then_inc(last["gate1"], 1)
                dve.wait_ge(last["gate1"], w + 1)
                nc.vector.reciprocal(gate_l[:, cols], gate_l[:, cols]).then_inc(last["gate"], 1)
            for w, cols in groups:
                dve.wait_ge(last["v_projected"], w + 1)
                dve.wait_ge(last["gate"], w + 1)
                nc.vector.tensor_tensor(y1_l[:, cols], ps_s[1][:, cols], gate_l[:, cols], ALU.mult)\
                    .then_inc(last["y2"], 1)
                dve.wait_ge(last["y2"], w + 1)
                nc.vector.tensor_tensor(y3_l[:, cols], y1_l[:, cols], x1_l[:, cols], ALU.add)\
                    .then_inc(last["y3"], 1)
                dve.wait_ge(last["y3"], w + 1)
                norm_stats(1, w, y3_l)
            for w, cols in groups:
                normed(1, w, y3_l, o_l, last["out"])

        @block.tensor
        def _(pe):
            pe.wait_ge(s_const, 2)
            pe.wait_ge(s_in_rpe, 16)
            for a in range(2):
                ins = nc.tensor.transpose(ps_t[0][:, HEADS * a:HEADS * a + HEADS],
                                          pt[0][0][0:HEADS, 0, P * a:P * a + P], ident[0:HEADS, 0:HEADS])
            ins.then_inc(s_rpe_t, 1)

            def transpose_x(b):
                pe.wait_ge(s_in_x, 16 if b == 0 else 32)
                if b > 0:
                    pe.wait_ge(s_xt, b)
                if b == 1:
                    pe.wait_ge(s_load, 32)
                for t in range(TILES):
                    ins = nc.tensor.transpose(ps_s[0][:, P * t:P * t + P], x_in[:, TILES * b + t, :], ident[:, :])
                ins.then_inc(s_setup_t, 1)

            transpose_x(0)

            def wait_chunk(m, c):
                if 0 <= c < 4:
                    pe.wait_ge(s_lo, 4 * m + c + 1)
                else:
                    pe.wait_ge(s_v, 2 * m + (c - 3 if c > 0 else 0))

            def wait_tile(e, matmuls):
                if matmuls in (0, 1):
                    pe.wait_ge(s_chain, CH * (e + matmuls) + (9 if matmuls == 0 else 1))
                elif matmuls == 2:
                    pe.wait_ge(s_x1t, e + 1)
                elif matmuls == 3:
                    pe.wait_ge(s_sig, e + 1)
                else:
                    pe.wait_ge(s_chain, CH * (e + 1) + 9)

            def project(m, c, tile_too):
                if c == 0:
                    pe.wait_ge(s_load, 32 * m + 32)
                if not (isinstance(m, int) and m == 0):
                    wait_chunk(m, c - 1)
                elif c >= 4:
                    wait_chunk(m, c - 4)
                if tile_too:
                    wait_tile(m - 1 - TILE_LAG, sum(at < PROJ_SLOTS[c] for at in TILE_MATMULS))
                if c < 4:
                    ins = nc.tensor.matmul(proj_bank(m, c), w_cur[:, c // 2, :], x_cur[:, 512 * (c % 2):512 * (c % 2) + 512],
                                           start=True, stop=True)
                else:
                    for t in range(4):
                        at = P * (4 * (c - 4) + t)
                        ins = nc.tensor.matmul(proj_bank(m, c)[:, P * t:P * t + P], x_cur[:, at:at + P], w_cur[:, 2, :],
                                               start=True, stop=True)
                ins.then_inc(s_proj, 1)

            def score(n, r):
                h, i = ROWS[r]
                if isinstance(n, int) and n == 0 and i == 0:
                    pe.wait_ge(s_first[h], 96)
                elif i % GROUP == 0:
                    pe.wait_ge(s_stack[h], 96 * n + 96)
                pe.wait_ge(s_biased, NROWS * n + r + 3 - rows_since(r))
                for c0 in range(0, P * (i + 1), 512):
                    cols = slice(c0, c0 + max(256, min(512, P * (i + 1) - c0)))
                    for k_st in (kh_st[h], kl_st[h]):
                        ins = nc.tensor.matmul(ps_rows[:, score_at(r) + cols.start:score_at(r) + cols.stop], q_st[h][:, P * i:P * i + P], k_st[:, cols],
                                               start=(k_st is kh_st[h]), stop=(k_st is kl_st[h]))
                ins.then_inc(s_score, 1)

            def transpose(n, r):
                pe.wait_ge(s_norm, NROWS * n + r + 1)
                for k in (k for k in range(NBANKS) if BANKS[k][0] == r):
                    _, b0, nb = BANKS[k]
                    pe.wait_ge(s_ev[k % 2], NBANKS // 2 * n + k // 2 + 1)
                    for b in range(nb):
                        at = P * (b0 + b)
                        ins = nc.tensor.transpose(ps_t[k % 2][:, P * b:P * b + P], prob[:, r % PSLOTS, at:at + P],
                                                  ident[:, :])
                    ins.then_inc(s_tr, 1)

            def mix(n, g, j):
                if j == 0:
                    if g == 0:
                        pe.wait_ge(s_vcur, 16 * n + 16)
                    for which in range(2):
                        pe.wait_ge(s_ev[which], NBANKS // 2 * n + (4 if g == 0 else 12) + 1)
                    pe.wait_ge(s_o, 2 * n + g + 1)
                    lone(pe)
                last = GROUP * (g + 1) - 1
                c0 = P * max(0, j - GROUP * g)
                for h in range(2):
                    ins = nc.tensor.matmul(ps_o[D * h:D * h + D, c0:], v_cur[:, j, D * h:D * h + D],
                                           pt[h][g][:, j, c0:], start=(j == 0), stop=(j == last))
                if j == last:
                    ins.then_inc(s_pv, 1)

            def tile_step(n, slot, more=False):
                e = n - TILE_LAG
                if more and slot in TILE_MATMULS:
                    wait_chunk(n + 1, sum(at <= slot for at in PROJ_SLOTS) - 1)
                if slot in TILE_MATMULS:
                    wait_tile(e, TILE_MATMULS.index(slot))
                if slot == OUT_PROJ:
                    pe.wait_ge(s_mixt, 16 * e + 16)
                    for p in range(PAIRS):
                        ins = nc.tensor.matmul(ps_m[:, 0:C], mix_tile[:, p, :], wo[:, p, :],
                                               start=(p == 0), stop=(p == PAIRS - 1))
                    ins.then_inc(s_e1, 1)
                if slot == X1_T:
                    pe.wait_ge(s_chain, CH * (e + 1) + 4)
                    nc.tensor.transpose(ps_m[:, 0:P], x1[:, :], ident[:, :]).then_inc(s_e4, 1)
                if slot == RK_PROJ:
                    pe.wait_ge(s_chain, CH * (e + 1) + 6)
                    nc.tensor.matmul(ps_m[:, 0:P], xr_t[:, :], w_t[:, 0, :], start=True, stop=True)
                    nc.tensor.matmul(ps_m[:, P:2 * P], w_t[:, 1, :], xk_t[:, :], start=True, stop=True)\
                        .then_inc(s_e6, 1)
                if slot == V_PROJ:
                    pe.wait_ge(s_chain, CH * (e + 1) + 7)
                    nc.tensor.matmul(ps_m[:, 0:C], k_act[:, :], w_t[:, 2, :], start=True, stop=True).then_inc(s_e8, 1)

            pe.sem_inc(s_tr, NBANKS)
            pe.sem_inc(s_pv, 2)
            for c in range(NPROJ):
                project(0, c, False)
                if c == 0:
                    pe.wait_ge(s_rpe_t, 2)
                    pe.wait_ge(s_const, 4)
                    for a in range(2):
                        ins = nc.tensor.matmul(ps_t[1][0:HEADS, :], rpe_t[:, a, :], upper[:, a, :],
                                               start=(a == 0), stop=(a == 1))
                    ins.then_inc(s_seq_mm, 1)
                if c % 2:
                    transpose_x(1 + c // 2)
            pe.wait_ge(s_in_w, 64)
            for a in range(3):
                ins = nc.tensor.transpose(ps_t[0][:, P * a:P * a + P], w_raw[:, a, :], ident[:, :])
            ins.then_inc(s_wt, 1)
            pe.wait_ge(s_xt, BATCH)
            pe.wait_ge(s_wt, 2)

            for r in range(LEAD):
                score(0, r)

            def step(n, prev, tile_too, more):
                for slot in range(NROWS):
                  for o in PE_ORDER:
                    if o == 'p' and more and slot in PROJ_SLOTS:
                        project(n + 1, PROJ_SLOTS.index(slot), tile_too)
                    if o == 's':
                      for row in rows_ahead(n, more, slot):
                        score(*row)
                    if o == 'e' and tile_too:
                        tile_step(n, slot, more)
                    if o == 'f' and prev and 0 <= slot - MIX_FAR < TILES:
                        mix(n - 1, 1, slot - MIX_FAR)
                    if o == 'm' and 0 <= slot - MIX_NEAR < GROUP:
                        mix(n, 0, slot - MIX_NEAR)
                    if o == 't':
                        transpose(n, slot)

            drive(pe, step)

            def out_project(w):
                for t in range(WIDE * w, WIDE * (w + 1)):
                    for p in range(PAIRS - 1):
                        ins = nc.tensor.matmul(ps_s[0][:, P * t:P * t + P], mix_last[:, p, P * t:P * t + P],
                                               wo[:, p, :], start=(p == 0), stop=(p == PAIRS - 2))
                ins.then_inc(last["out_projected"], 1)

            groups = [(w, slice(WIDE * P * w, WIDE * P * (w + 1))) for w in range(TILES // WIDE)]
            tile_step(PAIR_STEPS, OUT_PROJ)
            for j in range(TILES):
                mix(PAIR_STEPS - 1, 1, j)
            tile_step(PAIR_STEPS, X1_T)
            pe.wait_ge(last["mix_loaded"], 16)
            pe.wait_ge(s_biased, NROWS * PAIR_STEPS + 2)
            out_project(0)
            tile_step(PAIR_STEPS, RK_PROJ)
            out_project(1)
            tile_step(PAIR_STEPS, V_PROJ)
            for w, cols in groups:
                pe.wait_ge(s_o, 2 * (PAIR_STEPS - 1) + w + 2)
                for t in range(WIDE):
                    ins = nc.tensor.matmul(ps_s[1][:, cols.start + P * t:cols.start + P * t + P],
                                           mix_sb[w][:, P * t:P * t + P], wo[:, PAIRS - 1, :], start=True, stop=True)
                ins.then_inc(last["pair_projected"], 1)
            for w, cols in groups:
                pe.wait_ge(last["x1"], w + 1)
                for t in range(WIDE * w, WIDE * (w + 1)):
                    ins = nc.tensor.transpose(ps_s[1][:, P * t:P * t + P], x1_l[:, P * t:P * t + P], ident[:, :])
                ins.then_inc(last["x1_transposed"], 1)
            for which in range(2):
                pe.wait_ge(s_ev[which], NBANKS // 2 * PAIR_STEPS + 1)
            for w, cols in groups:
                pe.wait_ge(last["xrk"], w + 1)
                for t in range(WIDE * w, WIDE * (w + 1)):
                    nc.tensor.matmul(ps_s[0][:, P * t:P * t + P], xr_l[:, P * t:P * t + P], w_t[:, 0, :],
                                     start=True, stop=True)
                nc.tensor.matmul(ps_t[w][:, :], w_t[:, 1, :], xk_l[:, cols], start=True, stop=True)\
                    .then_inc(last["rk_projected"], 1)
            for w, cols in groups:
                pe.wait_ge(last["k_squared"], w + 1)
                for t in range(WIDE * w, WIDE * (w + 1)):
                    ins = nc.tensor.matmul(ps_s[1][:, P * t:P * t + P], k_l[:, P * t:P * t + P], w_t[:, 2, :],
                                           start=True, stop=True)
                ins.then_inc(last["v_projected"], 1)


_INS = ['L0_attn_x', 'L0_attn_qkv', 'L0_attn_out_w', 'L0_attn_rpe_bias', 'L0_ffn_W_r', 'L0_ffn_W_k', 'L0_ffn_W_v',
        'L0_ffn_mu_r', 'L0_ffn_mu_k']


def kernel(**inputs):
    import numpy as _np
    import concourse.bacc as _bacc
    from concourse import mybir as _mybir
    from concourse.bass_utils import run_bass_kernel_spmd as _run

    nc = _bacc.Bacc("TRN2", target_bir_lowering=False, num_devices=1)
    arrays, args = {}, []
    for name in _INS:
        a = _np.ascontiguousarray(inputs[name])
        arrays[f"in_{name}"] = a
        args.append(nc.dram_tensor(f"in_{name}", a.shape, _mybir.dt.from_np(a.dtype), kind="ExternalInput").ap())
    shape = inputs['L0_attn_x'].shape
    args.append(nc.dram_tensor("out_y", shape, _mybir.dt.float32, kind="ExternalOutput").ap())
    build(nc, *args)
    r = _run(nc, [arrays], core_ids=[0])
    return r.results[0]["out_y"]
```

```python
import concourse.bass as bass
from concourse import mybir
from contextlib import ExitStack

F32 = mybir.dt.float32
F32R = mybir.dt.float32r
ALU = mybir.AluOpType
ACT = mybir.ActivationFunctionType

BATCH, SEQ, C = 4, 1024, 128
HEADS, D, SPAN = 16, 64, 256
P = 128
PAIRS = HEADS // 2
PAIR_STEPS = BATCH * PAIRS
TILES = SEQ // P
GROUP = 4
NEAR = SPAN + P
FAR = SEQ - NEAR
BANK = 512
SHORTEST = 256
MASKED = 30000.0
EPS = 1e-5
SCALE = -(D ** -0.5)

ROWS = [(h, i) for g in range(TILES // GROUP) for h in range(2) for i in range(GROUP * g, GROUP * g + GROUP)]
NROWS = len(ROWS)
LEAD = 4
PSLOTS = 8


def bank_list():
    out = []
    for r, (_, i) in enumerate(ROWS):
        for b0 in range(0, i + 1, 4):
            out.append((r, b0, min(4, i + 1 - b0)))
    return out


def score_at(r):
    if r < NROWS // 2:
        return BANK * (r % 4)
    width = P * (ROWS[r][1] + 1)
    return SEQ * (r % 2) + ((SEQ - width) // 2 if width - BANK < SHORTEST else 0)


def score_end(r):
    return score_at(r) + P * (ROWS[r][1] + 1 if ROWS[r][1] >= GROUP else GROUP)


def rows_since(r):
    return next(k for k in range(1, NROWS)
                if score_at((r - k) % NROWS) < score_end(r) and score_at(r) < score_end((r - k) % NROWS))


BANKS = bank_list()
NBANKS = len(BANKS)
EVACUATOR = "010110010100010111110111"


def evacuated(engine, k):
    return sum(int(c) == engine for c in EVACUATOR[:k + 1])


EVACUATED = [evacuated(engine, NBANKS) for engine in range(2)]
PROJ_SLOTS = (2, 3, 5, 7, 10, 14)
NPROJ = len(PROJ_SLOTS)
OUT_PROJ, LN1_RSTD, LN1 = 0, 1, 2
X1_T, SHIFT = 4, 4
RK_PROJ, GATE = 9, 11
V_PROJ, LN2_RSTD, LN2 = 12, 13, 13
TILE_MATMULS = (OUT_PROJ, X1_T, RK_PROJ, V_PROJ)
WIDE = 4
MIX_FAR = 0
MIX_NEAR = 11
TILE_LAG = PAIRS + 1
CH = 13


def build(nc, x, qkv, out_w, rpe, w_r, w_k, w_v, mu_r, mu_k, out):
    seq_d = nc.dram_tensor("bias_by_distance", (HEADS, P, 4 * P), F32, kind="Internal").ap()
    toeplitz = bass.AP(seq_d.tensor, P - 1, [[P * 4 * P, HEADS], [4 * P - 1, P], [1, NEAR]])
    mix_d = nc.dram_tensor("mix_transposed", (PAIR_STEPS, P, SEQ), F32, kind="Internal").ap()
    xt_d = nc.dram_tensor("x_transposed", (BATCH, P, SEQ), F32, kind="Internal").ap()

    x_tiles = x.rearrange("b (t p) c -> p (b t) c", p=P)
    x_rows = x.rearrange("b s c -> (b s) c")
    out_rows = out.rearrange("b s c -> (b s) c")
    qkv_pairs = qkv.rearrange("c m (r h) d -> r c m (h d)", h=2)
    wo_pairs = out_w.rearrange("(r h) d c -> (h d) r c", h=2)

    with ExitStack() as ctx:
        def sb(name, shape, dt=F32):
            return ctx.enter_context(nc.sbuf_tensor(name, shape, dt))

        def ps(name, shape):
            return ctx.enter_context(nc.psum_tensor(name, shape, F32))

        def sem(name):
            return ctx.enter_context(nc.semaphore(name))

        ident = sb("ident", [P, P])
        wo = sb("wo", [P, PAIRS, C])
        w_t = sb("w_t", [P, 3, C])
        mu = sb("mu", [P, 4])
        eps = sb("eps", [P, 1])
        one = sb("one", [P, 1])
        x_cur = sb("x_cur", [P, SEQ])
        w_cur = sb("w_cur", [P, 3, P])
        q_hi, q_lo, k_hi, k_lo = (sb(n, [P, SEQ], F32R) for n in ("q_hi", "q_lo", "k_hi", "k_lo"))
        v_new = sb("v_new", [P, 2, TILES, P])
        q_st = [sb(f"q_st{h}", [P, SEQ], F32R) for h in range(2)]
        kh_st = [sb(f"kh_st{h}", [P, SEQ], F32R) for h in range(2)]
        kl_st = [sb(f"kl_st{h}", [P, SEQ], F32R) for h in range(2)]
        v_cur = sb("v_cur", [P, TILES, P])
        table = sb("table", [P, 2, SEQ])
        prob = sb("prob", [P, PSLOTS, SEQ])
        low = sb("low", [P, NROWS])
        total = sb("total", [P, NROWS])
        inv = sb("inv", [P, NROWS])
        pt = [[sb(f"pt{h}{g}", [P, GROUP * (g + 1), GROUP * P]) for g in range(2)] for h in range(2)]
        mix_sb = [sb(f"mix_sb{g}", [P, GROUP * P]) for g in range(2)]
        mix_tile = sb("mix_tile", [P, PAIRS, P])
        x_res = sb("x_res", [P, C])
        y1 = sb("y1", [P, C])
        o_tile = sb("o_tile", [P, C])
        x1 = sb("x1", [P, C])
        x1_t = sb("x1_t", [P, 1 + SEQ])
        shift = sb("shift", [P, 2, P])
        xr_t = sb("xr_t", [P, P])
        xk_t = sb("xk_t", [P, P])
        gate1, k_act, y2 = xr_t, xk_t, y1
        y3, gate = shift[:, 0, :], shift[:, 1, :]
        stats = sb("stats", [P, 2, 6])
        mv = sb("mv", [P, 2, 2])
        lnv = sb("lnv", [P, 2])
        rstd = sb("rstd", [P, 2])

        mix_last = sb("mix_last", [P, PAIRS - 1, SEQ])
        x_last = x_cur[:, :].rearrange("p (t c) -> p t c", c=C)
        y1_l, x1_l, shr_l, shk_l, xr_l, xk_l, gate_l, k_l = (prob[:, k, :] for k in range(8))
        y3_l, o_l = shr_l, shk_l
        stats_l = sb("stats_last", [P, 2, TILES, 6])
        mv_l = sb("mv_last", [P, 2, TILES, 2])
        lnv_l = sb("lnv_last", [P, 2, TILES])
        rstd_l = sb("rstd_last", [P, 2, TILES])

        x_t = mix_last[:, 0:BATCH, :].rearrange("p b s -> p (b s)")
        x_in = prob[:, 0:BATCH, :].rearrange("p a (t c) -> p (a t) c", c=C)
        rpe_in = pt[0][0][0:HEADS, 0, 0:SPAN]
        rpe_t = pt[0][0][:, 1, 0:2 * HEADS].rearrange("p (a n) -> p a n", a=2)
        upper = pt[1][0][:, 0:2, :]
        w_raw = pt[1][1][:, 0, 0:3 * C].rearrange("p (a c) -> p a c", a=3)
        seq_sb = x1_t[0:HEADS, 1:1 + 4 * P]

        ps_rows = ps("ps_rows", [P, 2 * SEQ])
        ps_s = [ps_rows[:, SEQ * k:SEQ * k + SEQ] for k in range(2)]
        ps_t = [ps(f"ps_t{k}", [P, 4 * P]) for k in range(2)]
        ps_o = ps("ps_o", [P, GROUP * P])
        ps_m = ps("ps_m", [P, 4 * P])

        s_in_x, s_in_w, s_in_rpe, s_in_mu = sem("in_x"), sem("in_w"), sem("in_rpe"), sem("in_mu")
        s_const = sem("const")
        s_zero = sem("zero")
        s_setup_t = sem("setup_transposed")
        s_xt = sem("xt_copied")
        s_wt = sem("wt_copied")
        s_rpe_t = sem("rpe_t")
        s_seq_mm = sem("seq_matmul")
        s_seq = sem("seq_ready")
        s_seq_dram = sem("seq_in_dram")
        s_xt_dram = sem("xt_in_dram")
        s_mu = sem("mu_ready")
        s_load = sem("pair_loaded")
        s_proj = sem("projected")
        s_hi = sem("hi_ready")
        s_lo = sem("lo_ready")
        s_v = sem("v_ready")
        s_first = [sem(f"first_half{h}") for h in range(2)]
        s_stack = [sem(f"stacked{h}") for h in range(2)]
        s_table = [sem(f"table{h}") for h in range(2)]
        s_vcur = sem("v_cur_loaded")
        s_score = sem("scored")
        s_biased = sem("biased")
        s_exp = sem("exped")
        s_inv = sem("inverted")
        s_norm = sem("normalised")
        s_tr = sem("transposed")
        s_ev = [sem("evacuated_dve"), sem("evacuated_act")]
        s_pv = sem("mixed")
        s_o = sem("mix_evacuated")
        s_mix_d = [sem(f"mix_in_dram{g}") for g in range(2)]
        s_xres, s_mixt = sem("x_res_loaded"), sem("mix_tile_loaded")
        s_e1, s_e4, s_e6, s_e8 = sem("out_projected"), sem("x1_transposed"), sem("rk_projected"), sem("v_projected")
        s_chain = sem("tile_chain")
        s_ln = sem("log_var")
        s_rstd = sem("rstd_ready")
        s_x1t = sem("x1_t_ready")
        s_sig = sem("exp_gate")
        s_store = sem("stored")
        s_own = sem("own_instruction")
        last = {k: sem(f"last_{k}") for k in (
            "x_loaded", "mix_loaded", "out_projected", "pair_projected", "part1", "y1", "stats1", "mv1", "ln1",
            "rstd1", "x1", "x1_transposed", "x1_t", "shifted", "xrk", "rk_projected", "relu_k", "k_squared", "gate", "log_gate",
            "v_projected", "y2", "y3", "stats2", "mv2", "ln2", "rstd2", "out", "stored")}

        def lone(e):
            e.sem_inc(s_own, 1)

        def drive(e, step, before_tiles=lambda: None):
            step(0, prev=False, tile_too=False, more=True)
            with e.Fori(1, TILE_LAG) as n:
                step(n, prev=True, tile_too=False, more=True)
            before_tiles()
            with e.Fori(TILE_LAG, PAIR_STEPS - 1) as n:
                step(n, prev=True, tile_too=True, more=True)
            step(PAIR_STEPS - 1, prev=True, tile_too=True, more=False)

        def proj_bank(m, c):
            if isinstance(m, int) and m == 0:
                return (ps_m[:, :], ps_o[:, :], ps_s[1][:, 0:512], ps_s[1][:, 512:])[c % 4]
            return ps_m[:, :]

        def chunk_of(m, c):
            return (c % 2, c // 2) if isinstance(m, int) and m == 0 else (c // 2, c % 2)

        def columns(w):
            return slice(WIDE * P * w, WIDE * P * (w + 1))

        def rows_ahead(n, more, slot):
            if slot + LEAD < NROWS:
                return [(n, slot + LEAD)]
            return [(n + 1, slot + LEAD - NROWS)] if more else []

        block = ctx.enter_context(nc.Block())

        @block.sync
        def _(sp):
            sp.dma_start(x_in[:, 0:TILES, :], x_tiles[:, 0:TILES, :]).then_inc(s_in_x, 16)
            sp.dma_start(rpe_in, rpe).then_inc(s_in_rpe, 16)
            sp.dma_start(w_cur[:, :, :], qkv_pairs[0, :, :, :]).then_inc(s_load, 16)
            sp.dma_start(x_in[:, TILES:, :], x_tiles[:, TILES:, :]).then_inc(s_in_x, 16)
            for n, w in enumerate((w_r, w_k, w_v)):
                sp.dma_start(w_raw[:, n, :], w).then_inc(s_in_w, 16)
            sp.dma_start(wo[:, :, :], wo_pairs).then_inc(s_in_w, 16)
            for n, m in enumerate((mu_r, mu_k)):
                sp.dma_start(mu[:, n:n + 1], m.rearrange("(c a) -> c a", a=1)).then_inc(s_in_mu, 16)

            def stack(h, done, cols=slice(0, SEQ)):
                own = slice(D * h, D * h + D)
                for dst, top, bottom in ((q_st[h], q_hi, q_lo), (kh_st[h], k_hi, k_hi), (kl_st[h], k_lo, k_lo)):
                    sp.dma_start(dst[0:D, cols].bitcast(F32), top[own, cols].bitcast(F32)).then_inc(done, 16)
                    sp.dma_start(dst[D:P, cols].bitcast(F32), bottom[own, cols].bitcast(F32)).then_inc(done, 16)

            sp.wait_ge(s_lo, 2)
            stack(0, s_first[0], slice(0, SEQ // 2))
            sp.wait_ge(s_seq, 2)
            copies = seq_sb.unsqueeze(1).broadcast_to([HEADS, P, 4 * P])
            sp.dma_start(seq_d[0:2, :, :], copies[0:2, :, :]).then_inc(s_seq_dram, 16)
            stack(1, s_first[1], slice(0, SEQ // 2))
            sp.wait_ge(s_seq_dram, 16)
            sp.wait_ge(s_zero, 1)
            for h in range(2):
                sp.dma_start(table[:, h, FAR:], toeplitz[h, :, :]).then_inc(s_table[h], 16)
            sp.wait_ge(s_proj, NPROJ)
            sp.sem_inc(s_load, 16)
            sp.dma_start(w_cur[:, :, :], qkv_pairs[1, :, :, :]).then_inc(s_load, 16)
            sp.wait_ge(s_lo, 4)
            stack(0, s_stack[0], slice(SEQ // 2, SEQ))
            sp.wait_ge(s_v, 2)
            sp.dma_start(v_cur[:, :, :], v_new[:, 0, :, :]).then_inc(s_vcur, 16)
            stack(1, s_stack[1], slice(SEQ // 2, SEQ))
            sp.dma_start(seq_d[2:, :, :], copies[2:, :, :]).then_inc(s_seq_dram, 16)
            sp.wait_ge(s_xt, BATCH)
            sp.dma_start(xt_d.rearrange("b c s -> c b s"), mix_last[:, 0:BATCH, :]).then_inc(s_xt_dram, 16)
            sp.wait_ge(s_seq_dram, 32)
            sp.wait_ge(s_xt_dram, 16)

            def loads(m):
                sp.wait_ge(s_proj, NPROJ * m)
                lone(sp)
                sp.dma_start(w_cur[:, :, :], qkv_pairs[bass.ds(m % PAIRS, 1), :, :, :]).then_inc(s_load, 16)
                sp.dma_start(x_cur[:, :], xt_d[bass.ds(m // PAIRS % BATCH, 1), :, :]).then_inc(s_load, 16)

            def store_mix(n, g):
                sp.wait_ge(s_o, 2 * n + g + 2)
                lone(sp)
                sp.dma_start(mix_d[bass.ds(n, 1), :, GROUP * P * g:GROUP * P * (g + 1)], mix_sb[g][:, :])\
                    .then_inc(s_mix_d[g], 16)

            def tile_loads(n, pairs=0):
                sp.wait_ge(s_chain, CH * (n - TILE_LAG) + 1)
                lone(sp)
                sp.dma_start(x_res[:, :], x_rows[bass.ds((n - TILE_LAG) * P, P), :]).then_inc(s_xres, 16)
                for g in range(2):
                    sp.wait_ge(s_mix_d[g], 16 * (pairs or n - 1) + 16)
                    lone(sp)
                tiles = mix_d.rearrange("(b r) d (t s) -> b t d r s", r=PAIRS, s=P)
                e = n - TILE_LAG
                sp.dma_start(mix_tile[:, :, :], tiles[bass.ds(e // TILES, 1), bass.ds(e % TILES, 1), :, :, :])\
                    .then_inc(s_mixt, 16)

            def load_mix_last(first, end):
                for g in range(2):
                    sp.wait_ge(s_mix_d[g], 16 * (PAIR_STEPS - PAIRS + end) + 16)
                sp.dma_start(mix_last[:, first:end, :], mix_d[PAIR_STEPS - PAIRS + first:PAIR_STEPS - PAIRS + end, :, :]
                             .rearrange("r d s -> d r s")).then_inc(last["mix_loaded"], 16)

            def tile_store(n):
                sp.wait_ge(s_chain, CH * (n - TILE_LAG) + 2 * CH)
                lone(sp)
                sp.dma_start(out_rows[bass.ds((n - TILE_LAG) * P, P), :], o_tile[:, :]).then_inc(s_store, 16)

            def restack(n, h):
                rows = NROWS - GROUP * (1 - h)
                sp.wait_ge(s_score, NROWS * n + rows)
                stack(h, s_stack[h])
                sp.wait_ge(s_biased, NROWS * n + rows + 2)
                lone(sp)
                sp.dma_start(table[:, h, FAR:],
                             toeplitz[bass.ds((n + 1) % PAIRS * 2 + h, 1), :, :]).then_inc(s_table[h], 16)

            def step(n, prev, tile_too, more):
                if prev:
                    sp.wait_ge(s_v, 2 * n + 2)
                    sp.wait_ge(s_pv, 2 * n + 2)
                    lone(sp)
                    sp.dma_start(v_cur[:, :, :], v_new[:, bass.ds(n % 2, 1), :, :]).then_inc(s_vcur, 16)
                if more:
                    sp.wait_ge(s_lo, 4 * n + 8)
                    lone(sp)
                    restack(n, 0)
                if not more:
                    sp.wait_ge(s_proj, NPROJ * PAIR_STEPS)
                    sp.wait_ge(s_load, 32 * (PAIR_STEPS + 1))
                    sp.dma_start(x_last, x_tiles[:, TILES * (BATCH - 1):, :]).then_inc(last["x_loaded"], 16)
                    tile_loads(PAIR_STEPS, pairs=PAIR_STEPS - PAIRS)
                    load_mix_last(0, PAIRS - 2)
                if prev:
                    store_mix(n - 1, 1)
                if more:
                    restack(n, 1)
                if tile_too and more:
                    tile_loads(n + 1)
                if more:
                    loads(n + 2)
                else:
                    load_mix_last(PAIRS - 2, PAIRS - 1)
                if tile_too:
                    tile_store(n)
                if more:
                    store_mix(n, 0)

            drive(sp, step, before_tiles=lambda: tile_loads(TILE_LAG))
            tile_store(PAIR_STEPS)
            for w in range(TILES // WIDE):
                sp.wait_ge(last["out"], w + 1)
                sp.dma_start(out.rearrange("b (t p) c -> b p t c", p=P)[BATCH - 1, :, WIDE * w:WIDE * (w + 1), :],
                             o_l[:, WIDE * P * w:WIDE * P * (w + 1)].rearrange("p (t c) -> p t c", c=C))\
                    .then_inc(last["stored"], 16)
            sp.wait_ge(last["stored"], 16 * TILES // WIDE)
            sp.wait_ge(s_store, 16 * (BATCH - 1) * TILES + 16)

        @block.gpsimd
        def _(pool):
            pool.memset(ident[:, :], 0.0).then_inc(s_const, 1)
            pool.wait_ge(s_const, 1)
            pool.affine_select(out=ident[:, :], in_=ident[:, :], compare_op=ALU.not_equal, fill=1.0, base=0,
                               pattern=[[-1, P]], channel_multiplier=1).then_inc(s_const, 1)
            pool.memset(upper, 1.0).then_inc(s_const, 1)
            pool.wait_ge(s_const, 3)
            pool.affine_select(out=upper, in_=upper, compare_op=ALU.is_gt, fill=0.0, base=-(NEAR - 1),
                               pattern=[[P, 2], [1, 4 * P]], channel_multiplier=1).then_inc(s_const, 1)
            pool.memset(table[:, :, 0:FAR], 0.0).then_inc(s_zero, 1)
            pool.memset(x1_t[:, 0:1], 0.0).then_inc(s_zero, 1)
            pool.memset(eps[:, :], EPS).then_inc(s_zero, 1)
            pool.memset(one[:, :], 1.0).then_inc(s_zero, 1)

            def normalise(n, r):
                width = P * (ROWS[r][1] + 1)
                pool.wait_ge(s_inv, NROWS * n + r + 1)
                row = prob[:, r % PSLOTS, 0:width]
                nc.gpsimd.tensor_tensor(row, row, inv[:, r:r + 1].broadcast_to([P, width]), ALU.mult)\
                    .then_inc(s_norm, 1)

            with pool.Fori(0, PAIR_STEPS) as n:
                for r in range(NROWS):
                    normalise(n, r)
            for w in range(TILES // WIDE):
                cols = columns(w)
                pool.wait_ge(last["relu_k"], w + 1)
                nc.gpsimd.tensor_tensor(k_l[:, cols], k_l[:, cols], k_l[:, cols], ALU.mult)\
                    .then_inc(last["k_squared"], 1)

        @block.scalar
        def _(act):
            nc.scalar.preload_act_table_set("natural_log_exp_and_others")

            def copy_x(b):
                act.wait_ge(s_setup_t, b + 1)
                if b == 0:
                    act.wait_ge(s_load, 32)
                nc.scalar.activation(x_t[:, SEQ * b:SEQ * b + SEQ], ps_s[0], ACT.Copy).then_inc(s_xt, 1)

            def project(m, c):
                if c == 0 and not (isinstance(m, int) and m == 0):
                    for h in range(2):
                        if isinstance(m, int):
                            act.wait_ge(s_first[h], 96)
                        act.wait_ge(s_stack[h], 96 * m)
                act.wait_ge(s_proj, NPROJ * m + c + 1)
                if c < 4:
                    which, at = chunk_of(m, c)
                    dst, scale = ((q_hi, SCALE), (k_hi, 1.0))[which]
                    half = slice(512 * at, 512 * at + 512)
                    nc.scalar.activation(dst[:, half], proj_bank(m, c), ACT.Copy, scale=scale).then_inc(s_hi, 1)
                else:
                    half = slice(4 * (c - 4), 4 * (c - 4) + 4)
                    if c == 4 and not (isinstance(m, int) and m < 2):
                        act.wait_ge(s_vcur, 16 * m - 16)
                    lone(act)
                    nc.scalar.activation(v_new[:, bass.ds(m % 2, 1), half, :],
                                         proj_bank(m, c).rearrange("p (a t d) -> p a t d", a=1, d=P),
                                         ACT.Copy).then_inc(s_v, 1)

            def exps(n, r):
                width = P * (ROWS[r][1] + 1)
                act.wait_ge(s_biased, NROWS * n + r + 3)
                row = prob[:, r % PSLOTS, 0:width]
                nc.scalar.activation(row, row, ACT.Exp, bias=low[:, r:r + 1], scale=-1.0,
                                     accum_out=total[:, r:r + 1]).then_inc(s_exp, 1)

            def evacuate(n, k):
                r, b0, nb = BANKS[k]
                h, i = ROWS[r]
                g = i // GROUP
                act.wait_ge(s_pv, 2 * n + g + 1)
                act.wait_ge(s_tr, NBANKS * (n + 1) + k + 1)
                nc.scalar.activation(pt[h][g][:, b0:b0 + nb, P * (i % GROUP):P * (i % GROUP) + P],
                                     ps_t[k % 2][:, 0:nb * P].rearrange("p (b s) -> p b s", s=P),
                                     ACT.Copy).then_inc(s_ev[1], 1)

            def tile_step(n, slot):
                e = n - TILE_LAG
                for which, at in ((0, LN1_RSTD), (1, LN2_RSTD)):
                    if slot == at:
                        act.wait_ge(s_chain, CH * (e + 1) + (3 if which == 0 else 12))
                        nc.scalar.activation(lnv[:, which:which + 1], mv[:, which, 1:2], ACT.Ln,
                                             bias=eps[:, 0:1]).then_inc(s_ln, 1)
                        act.wait_ge(s_ln, 2 * e + which + 1)
                        nc.scalar.activation(rstd[:, which:which + 1], lnv[:, which:which + 1], ACT.Exp,
                                             scale=-0.5).then_inc(s_rstd, 1)
                if slot == X1_T:
                    act.wait_ge(s_e4, e + 1)
                    lone(act)
                    nc.scalar.activation(x1_t[:, bass.ds(1 + (n - TILE_LAG) % TILES * P, P)], ps_m[:, 0:P], ACT.Copy)\
                        .then_inc(s_x1t, 1)
                if slot == RK_PROJ:
                    act.wait_ge(s_e6, e + 1)
                    nc.scalar.activation(gate, ps_m[:, 0:P], ACT.Exp, scale=-1.0)
                    nc.scalar.activation(k_act[:, :], ps_m[:, P:2 * P], ACT.Relu).then_inc(s_sig, 1)

            copy_x(0)
            for c in range(NPROJ):
                project(0, c)
                if c % 2:
                    copy_x(1 + c // 2)
            act.wait_ge(s_zero, 4)

            for r in range(LEAD):
                exps(0, r)

            def step(n, prev, tile_too, more):
                for slot in range(NROWS):
                    if more and slot in PROJ_SLOTS:
                        project(n + 1, PROJ_SLOTS.index(slot))
                    if tile_too:
                        tile_step(n, slot)
                    for k in range(NBANKS):
                        if BANKS[k][0] == slot and EVACUATOR[k] == "1":
                            evacuate(n, k)
                    for row in rows_ahead(n, more, slot):
                        exps(*row)

            drive(act, step)

            def ln_rstd(which, w):
                tiles = slice(WIDE * w, WIDE * (w + 1))
                act.wait_ge(last[f"mv{which + 1}"], w + 1)
                nc.scalar.activation(lnv_l[:, which, tiles], mv_l[:, which, tiles, 1], ACT.Ln, bias=eps[:, 0:1])\
                    .then_inc(last[f"ln{which + 1}"], 1)
                act.wait_ge(last[f"ln{which + 1}"], w + 1)
                nc.scalar.activation(rstd_l[:, which, tiles], lnv_l[:, which, tiles], ACT.Exp, scale=-0.5)\
                    .then_inc(last[f"rstd{which + 1}"], 1)

            def copy_x1(w):
                cols = columns(w)
                act.wait_ge(s_chain, CH * ((BATCH - 1) * TILES) + 6)
                act.wait_ge(last["x1_transposed"], w + 1)
                nc.scalar.activation(x1_t[:, 1 + cols.start:1 + cols.stop], ps_s[1][:, cols], ACT.Copy)\
                    .then_inc(last["x1_t"], 1)

            def relu_and_gate(w):
                cols = columns(w)
                act.wait_ge(last["rk_projected"], w + 1)
                nc.scalar.activation(k_l[:, cols], ps_t[w][:, :], ACT.Relu).then_inc(last["relu_k"], 1)
                nc.scalar.activation(gate_l[:, cols], ps_s[0][:, cols], ACT.Abs).then_inc(last["gate"], 1)
                act.wait_ge(last["gate"], 4 * w + 1)
                nc.scalar.activation(gate_l[:, cols], gate_l[:, cols], ACT.Exp, scale=-1.0).then_inc(last["gate"], 1)
                act.wait_ge(last["gate"], 4 * w + 2)
                nc.scalar.activation(gate_l[:, cols], gate_l[:, cols], ACT.Ln, bias=one[:, 0:1])\
                    .then_inc(last["gate"], 1)
                act.wait_ge(last["log_gate"], w + 1)
                nc.scalar.activation(gate_l[:, cols], gate_l[:, cols], ACT.Exp).then_inc(last["gate"], 1)

            tile_step(PAIR_STEPS, LN1_RSTD)
            ln_rstd(0, 0)
            tile_step(PAIR_STEPS, X1_T)
            copy_x1(0)
            ln_rstd(0, 1)
            tile_step(PAIR_STEPS, RK_PROJ)
            copy_x1(1)
            relu_and_gate(0)
            tile_step(PAIR_STEPS, LN2_RSTD)
            relu_and_gate(1)
            ln_rstd(1, 0)
            ln_rstd(1, 1)

        @block.vector
        def _(dve):
            dve.sem_inc(s_biased, 2)
            dve.sem_inc(s_ev[0], EVACUATED[0])
            dve.sem_inc(s_ev[1], EVACUATED[1])
            dve.sem_inc(s_o, 1)
            dve.sem_inc(s_chain, CH)
            dve.sem_inc(s_store, 16)
            dve.sem_inc(s_mix_d[0], 16)
            dve.sem_inc(s_mix_d[1], 16)
            nc.vector.memset(seq_sb[:, NEAR:], MASKED).then_inc(s_seq, 1)
            dve.wait_ge(s_setup_t, 1)
            for half in (slice(0, SEQ // 2), slice(SEQ // 2, SEQ)):
                nc.vector.tensor_copy(x_cur[:, half], ps_s[0][:, half]).then_inc(s_load, 8)
            dve.wait_ge(s_rpe_t, 1)
            nc.vector.tensor_copy(rpe_t, ps_t[0][:, 0:2 * HEADS].rearrange("p (a n) -> p a n", a=2)).then_inc(s_rpe_t, 1)

            def project(m, c):
                dve.wait_ge(s_hi, 4 * m + c + 1)
                which, at = chunk_of(m, c)
                hi, lo, scale = ((q_hi, q_lo, SCALE), (k_hi, k_lo, 1.0))[which]
                half = slice(512 * at, 512 * at + 512)
                nc.vector.scalar_tensor_tensor(out=lo[:, half], in0=proj_bank(m, c), scalar=scale,
                                               in1=hi[:, half].bitcast(F32), op0=ALU.mult, op1=ALU.subtract)\
                    .then_inc(s_lo, 1)

            def bias(n, r):
                h, i = ROWS[r]
                width = P * (i + 1)
                if i % GROUP == 0:
                    dve.wait_ge(s_table[h], 16 * n + 16)
                before = (r - PSLOTS) % NROWS
                dve.wait_ge(s_tr, NBANKS * (n if before > r else n + 1) + sum(b[0] <= before for b in BANKS))
                dve.wait_ge(s_score, NROWS * n + r + 1)
                lone(dve)
                nc.vector.tensor_tensor_reduce(prob[:, r % PSLOTS, 0:width],
                                               ps_rows[:, score_at(r):score_at(r) + width],
                                               table[:, h, SEQ - width:], 1.0, 3.0e38, ALU.add, ALU.min,
                                               low[:, r:r + 1]).then_inc(s_biased, 1)

            def invert(n, r):
                dve.wait_ge(s_exp, NROWS * n + r + 1)
                nc.vector.reciprocal(inv[:, r:r + 1], total[:, r:r + 1]).then_inc(s_inv, 1)

            def evacuate(n, k):
                r, b0, nb = BANKS[k]
                h, i = ROWS[r]
                g = i // GROUP
                dve.wait_ge(s_pv, 2 * n + g + 1)
                dve.wait_ge(s_tr, NBANKS * (n + 1) + k + 1)
                nc.vector.tensor_copy(pt[h][g][:, b0:b0 + nb, P * (i % GROUP):P * (i % GROUP) + P],
                                      ps_t[k % 2][:, 0:nb * P].rearrange("p (b s) -> p b s", s=P)).then_inc(s_ev[0], 1)

            def store_mix(n, g):
                dve.wait_ge(s_pv, 2 * n + g + 3)
                dve.wait_ge(s_mix_d[g], 16 * n + 16)
                nc.vector.tensor_copy(mix_sb[g][:, :], ps_o[:, :]).then_inc(s_o, 1)

            def tile_step(n, slot):
                e = n - TILE_LAG

                def link(ins, k):
                    ins.then_inc(s_chain, 1)
                    dve.wait_ge(s_chain, CH * (e + 1) + k)

                if slot == OUT_PROJ:
                    dve.wait_ge(s_e1, e + 1)
                    dve.wait_ge(s_xres, 16 * e + 16)
                    link(nc.vector.tensor_tensor(y1[:, :], ps_m[:, 0:C], x_res[:, :], ALU.add), 1)
                    link(nc.vector.bn_stats(stats[:, 0, :], y1[:, :]), 2)
                    lone(dve)
                    nc.vector.bn_aggr(mv[:, 0, :], stats[:, 0, :]).then_inc(s_chain, 1)
                if slot == LN1:
                    dve.wait_ge(s_rstd, 2 * e + 1)
                    nc.vector.tensor_scalar(x1[:, :], y1[:, :], mv[:, 0, 0:1], rstd[:, 0:1],
                                            ALU.subtract, ALU.mult).then_inc(s_chain, 1)
                if slot == SHIFT:
                    dve.wait_ge(s_x1t, e + 1)
                    for a in range(2):
                        ins = nc.vector.tensor_scalar(shift[:, a, :], x1_t[:, bass.ds((n - TILE_LAG) % TILES * P, P)],
                                                      mu[:, 2 + a:3 + a], None, ALU.mult)
                    link(ins, 5)
                    for a, dst in enumerate((xr_t, xk_t)):
                        own = x1_t[:, bass.ds(1 + (n - TILE_LAG) % TILES * P, P)]
                        ins = nc.vector.scalar_tensor_tensor(out=dst[:, :], in0=own, scalar=mu[:, a:a + 1],
                                                             in1=shift[:, a, :], op0=ALU.mult, op1=ALU.add)
                    ins.then_inc(s_chain, 1)
                if slot == RK_PROJ:
                    dve.wait_ge(s_sig, e + 1)
                    nc.vector.tensor_tensor(k_act[:, :], k_act[:, :], k_act[:, :], ALU.mult)
                    nc.vector.tensor_scalar(gate1[:, :], gate, 1.0, None, ALU.add).then_inc(s_chain, 1)
                if slot == GATE:
                    dve.wait_ge(s_chain, CH * (e + 1) + 7)
                    nc.vector.reciprocal(gate, gate1[:, :]).then_inc(s_chain, 1)
                if slot == V_PROJ:
                    dve.wait_ge(s_e8, e + 1)
                    dve.wait_ge(s_chain, CH * (e + 1) + 8)
                    link(nc.vector.tensor_tensor(y2[:, :], ps_m[:, 0:C], gate, ALU.mult), 9)
                    link(nc.vector.tensor_tensor(y3, y2[:, :], x1[:, :], ALU.add), 10)
                    link(nc.vector.bn_stats(stats[:, 1, :], y3), 11)
                    lone(dve)
                    nc.vector.bn_aggr(mv[:, 1, :], stats[:, 1, :]).then_inc(s_chain, 1)
                if slot == LN2:
                    dve.wait_ge(s_rstd, 2 * e + 2)
                    dve.wait_ge(s_store, 16 * e + 16)
                    nc.vector.tensor_scalar(o_tile[:, :], y3, mv[:, 1, 0:1], rstd[:, 1:2],
                                            ALU.subtract, ALU.mult).then_inc(s_chain, 1)

            for c in range(4):
                if c == 2:
                    dve.wait_ge(s_seq_mm, 1)
                    nc.vector.tensor_copy(seq_sb[:, 0:NEAR], ps_t[1][0:HEADS, 0:NEAR]).then_inc(s_seq, 1)
                project(0, c)
            dve.wait_ge(s_in_mu, 32)
            nc.vector.tensor_scalar(mu[:, 2:4], mu[:, 0:2], -1.0, 1.0, ALU.mult, ALU.add).then_inc(s_mu, 1)
            dve.wait_ge(s_wt, 1)
            nc.vector.tensor_copy(w_t[:, :, :], ps_t[0][:, 0:3 * P].rearrange("p (a n) -> p a n", a=3)).then_inc(s_wt, 1)

            for r in range(LEAD):
                bias(0, r)
                if r:
                    invert(0, r - 1)

            def step(n, prev, tile_too, more):
                for slot in range(NROWS):
                    for row in rows_ahead(n, more, slot):
                        bias(*row)
                    for row in rows_ahead(n, more, slot - 1):
                        invert(*row)
                    if more and slot in PROJ_SLOTS[:4]:
                        project(n + 1, PROJ_SLOTS.index(slot))
                    for k in range(NBANKS):
                        if BANKS[k][0] == slot and EVACUATOR[k] == "0":
                            evacuate(n, k)
                    if prev and slot == MIX_FAR + TILES:
                        store_mix(n - 1, 1)
                    if slot == MIX_NEAR + GROUP:
                        store_mix(n, 0)
                    if tile_too:
                        tile_step(n, slot)

            drive(dve, step)

            def add_residual(w):
                cols = columns(w)
                dve.wait_ge(s_tr, NBANKS * (PAIR_STEPS + 1))
                dve.wait_ge(last["x_loaded"], 16)
                dve.wait_ge(last["out_projected"], w + 1)
                nc.vector.tensor_tensor(y1_l[:, cols], ps_s[0][:, cols], x_cur[:, cols], ALU.add)\
                    .then_inc(last["part1"], 1)

            def each(w):
                return range(WIDE * w, WIDE * (w + 1))

            def norm_stats(which, w, y):
                for t in each(w):
                    ins = nc.vector.bn_stats(stats_l[:, which, t, :], y[:, P * t:P * t + P])
                ins.then_inc(last[f"stats{which + 1}"], 1)
                dve.wait_ge(last[f"stats{which + 1}"], w + 1)
                lone(dve)
                for t in each(w):
                    ins = nc.vector.bn_aggr(mv_l[:, which, t, :], stats_l[:, which, t, :])
                ins.then_inc(last[f"mv{which + 1}"], 1)

            def normed(which, w, y, dst, done):
                dve.wait_ge(last[f"rstd{which + 1}"], w + 1)
                for t in each(w):
                    ins = nc.vector.tensor_scalar(dst[:, P * t:P * t + P], y[:, P * t:P * t + P],
                                                  mv_l[:, which, t, 0:1], rstd_l[:, which, t:t + 1],
                                                  ALU.subtract, ALU.mult)
                ins.then_inc(done, 1)

            def add_last_pair(w):
                cols = columns(w)
                dve.wait_ge(last["pair_projected"], w + 1)
                dve.wait_ge(last["part1"], w + 1)
                nc.vector.tensor_tensor(y1_l[:, cols], ps_s[1][:, cols], y1_l[:, cols], ALU.add)\
                    .then_inc(last["y1"], 1)
                dve.wait_ge(last["y1"], w + 1)
                norm_stats(0, w, y1_l)

            def shift_tokens(w):
                cols = columns(w)
                dve.wait_ge(last["x1_t"], w + 1)
                for a, dst in enumerate((shr_l, shk_l)):
                    ins = nc.vector.tensor_scalar(dst[:, cols], x1_t[:, cols], mu[:, 2 + a:3 + a], None, ALU.mult)
                ins.then_inc(last["shifted"], 1)
                dve.wait_ge(last["shifted"], w + 1)
                for a, (dst, shifted) in enumerate(((xr_l, shr_l), (xk_l, shk_l))):
                    ins = nc.vector.scalar_tensor_tensor(out=dst[:, cols], in0=x1_t[:, 1 + cols.start:1 + cols.stop],
                                                         scalar=mu[:, a:a + 1], in1=shifted[:, cols],
                                                         op0=ALU.mult, op1=ALU.add)
                ins.then_inc(last["xrk"], 1)

            def log_gate(w):
                cols = columns(w)
                dve.wait_ge(last["gate"], 4 * w + 3)
                nc.vector.scalar_tensor_tensor(out=gate_l[:, cols], in0=ps_s[0][:, cols], scalar=0.0,
                                               in1=gate_l[:, cols], op0=ALU.min, op1=ALU.subtract)\
                    .then_inc(last["log_gate"], 1)

            def gated_sum(w):
                cols = columns(w)
                dve.wait_ge(last["v_projected"], w + 1)
                dve.wait_ge(last["gate"], 4 * w + 4)
                nc.vector.tensor_tensor(y1_l[:, cols], ps_s[1][:, cols], gate_l[:, cols], ALU.mult)\
                    .then_inc(last["y2"], 1)
                dve.wait_ge(last["y2"], w + 1)
                nc.vector.tensor_tensor(y3_l[:, cols], y1_l[:, cols], x1_l[:, cols], ALU.add)\
                    .then_inc(last["y3"], 1)
                dve.wait_ge(last["y3"], w + 1)
                norm_stats(1, w, y3_l)

            for slot in sorted({OUT_PROJ, LN1}):
                tile_step(PAIR_STEPS, slot)
            add_residual(0)
            add_last_pair(0)
            normed(0, 0, y1_l, x1_l, last["x1"])
            store_mix(PAIR_STEPS - 1, 1)
            tile_step(PAIR_STEPS, SHIFT)
            shift_tokens(0)
            add_residual(1)
            add_last_pair(1)
            normed(0, 1, y1_l, x1_l, last["x1"])
            for slot in sorted({RK_PROJ, GATE}):
                tile_step(PAIR_STEPS, slot)
            shift_tokens(1)
            log_gate(0)
            tile_step(PAIR_STEPS, V_PROJ)
            gated_sum(0)
            tile_step(PAIR_STEPS, LN2)
            log_gate(1)
            normed(1, 0, y3_l, o_l, last["out"])
            gated_sum(1)
            normed(1, 1, y3_l, o_l, last["out"])

        @block.tensor
        def _(pe):
            pe.wait_ge(s_const, 2)
            pe.wait_ge(s_in_rpe, 16)
            for a in range(2):
                ins = nc.tensor.transpose(ps_t[0][:, HEADS * a:HEADS * a + HEADS],
                                          pt[0][0][0:HEADS, 0, P * a:P * a + P], ident[0:HEADS, 0:HEADS])
            ins.then_inc(s_rpe_t, 1)

            def transpose_x(b):
                pe.wait_ge(s_in_x, 16 if b == 0 else 32)
                if b > 0:
                    pe.wait_ge(s_xt, b)
                if b == 1:
                    pe.wait_ge(s_load, 32)
                for t in range(TILES):
                    ins = nc.tensor.transpose(ps_s[0][:, P * t:P * t + P], x_in[:, TILES * b + t, :], ident[:, :])
                ins.then_inc(s_setup_t, 1)

            transpose_x(0)

            def wait_chunk(m, c):
                if 0 <= c < 4:
                    pe.wait_ge(s_lo, 4 * m + c + 1)
                else:
                    pe.wait_ge(s_v, 2 * m + (c - 3 if c > 0 else 0))

            def wait_tile(e, matmuls):
                if matmuls in (0, 1):
                    pe.wait_ge(s_chain, CH * (e + matmuls) + (9 if matmuls == 0 else 1))
                elif matmuls == 2:
                    pe.wait_ge(s_x1t, e + 1)
                elif matmuls == 3:
                    pe.wait_ge(s_sig, e + 1)
                else:
                    pe.wait_ge(s_chain, CH * (e + 1) + 9)

            def project(m, c, tile_too):
                if c == 0:
                    pe.wait_ge(s_load, 32 * m + 32)
                if not (isinstance(m, int) and m == 0):
                    wait_chunk(m, c - 1)
                elif c >= 4:
                    wait_chunk(m, c - 4)
                if tile_too:
                    wait_tile(m - 1 - TILE_LAG, sum(at < PROJ_SLOTS[c] for at in TILE_MATMULS))
                if c < 4:
                    which, at = chunk_of(m, c)
                    ins = nc.tensor.matmul(proj_bank(m, c), w_cur[:, which, :], x_cur[:, 512 * at:512 * at + 512],
                                           start=True, stop=True)
                else:
                    for t in range(4):
                        at = P * (4 * (c - 4) + t)
                        ins = nc.tensor.matmul(proj_bank(m, c)[:, P * t:P * t + P], x_cur[:, at:at + P], w_cur[:, 2, :],
                                               start=True, stop=True)
                ins.then_inc(s_proj, 1)

            def score(n, r):
                h, i = ROWS[r]
                if isinstance(n, int) and n == 0 and i == 0:
                    pe.wait_ge(s_first[h], 96)
                elif i % GROUP == 0:
                    pe.wait_ge(s_stack[h], 96 * n + 96)
                pe.wait_ge(s_biased, NROWS * n + r + 3 - rows_since(r))
                at, width = score_at(r), P * (i + 1)
                cut = BANK - at % BANK
                for c0, c1 in ((0, min(cut, width)), (cut, width)):
                    if c0 >= c1:
                        continue
                    c1 = max(c1, c0 + SHORTEST)
                    for k_st in (kh_st[h], kl_st[h]):
                        ins = nc.tensor.matmul(ps_rows[:, at + c0:at + c1], q_st[h][:, P * i:P * i + P],
                                               k_st[:, c0:c1], start=(k_st is kh_st[h]), stop=(k_st is kl_st[h]))
                ins.then_inc(s_score, 1)

            def transpose(n, r):
                pe.wait_ge(s_norm, NROWS * n + r + 1)
                for k in (k for k in range(NBANKS) if BANKS[k][0] == r):
                    _, b0, nb = BANKS[k]
                    engine = int(EVACUATOR[k - 2])
                    pe.wait_ge(s_ev[engine], EVACUATED[engine] * (n + (k >= 2)) + evacuated(engine, (k - 2) % NBANKS))
                    for b in range(nb):
                        at = P * (b0 + b)
                        ins = nc.tensor.transpose(ps_t[k % 2][:, P * b:P * b + P], prob[:, r % PSLOTS, at:at + P],
                                                  ident[:, :])
                    ins.then_inc(s_tr, 1)

            def mix(n, g, j):
                if j == 0:
                    if g == 0:
                        pe.wait_ge(s_vcur, 16 * n + 16)
                    for which in range(2):
                        last_bank = max(k for k in range(NBANKS) if ROWS[BANKS[k][0]][1] < GROUP * (g + 1))
                        pe.wait_ge(s_ev[which], EVACUATED[which] * (n + 1) + evacuated(which, last_bank))
                    pe.wait_ge(s_o, 2 * n + g + 1)
                    lone(pe)
                last = GROUP * (g + 1) - 1
                c0 = P * max(0, j - GROUP * g)
                for h in range(2):
                    ins = nc.tensor.matmul(ps_o[D * h:D * h + D, c0:], v_cur[:, j, D * h:D * h + D],
                                           pt[h][g][:, j, c0:], start=(j == 0), stop=(j == last))
                if j == last:
                    ins.then_inc(s_pv, 1)

            def tile_step(n, slot, more=False):
                e = n - TILE_LAG
                if more and slot in TILE_MATMULS:
                    wait_chunk(n + 1, sum(at <= slot for at in PROJ_SLOTS) - 1)
                if slot in TILE_MATMULS:
                    wait_tile(e, TILE_MATMULS.index(slot))
                if slot == OUT_PROJ:
                    pe.wait_ge(s_mixt, 16 * e + 16)
                    for p in range(PAIRS):
                        ins = nc.tensor.matmul(ps_m[:, 0:C], mix_tile[:, p, :], wo[:, p, :],
                                               start=(p == 0), stop=(p == PAIRS - 1))
                    ins.then_inc(s_e1, 1)
                if slot == X1_T:
                    pe.wait_ge(s_chain, CH * (e + 1) + 4)
                    nc.tensor.transpose(ps_m[:, 0:P], x1[:, :], ident[:, :]).then_inc(s_e4, 1)
                if slot == RK_PROJ:
                    pe.wait_ge(s_chain, CH * (e + 1) + 6)
                    nc.tensor.matmul(ps_m[:, 0:P], xr_t[:, :], w_t[:, 0, :], start=True, stop=True)
                    nc.tensor.matmul(ps_m[:, P:2 * P], w_t[:, 1, :], xk_t[:, :], start=True, stop=True)\
                        .then_inc(s_e6, 1)
                if slot == V_PROJ:
                    pe.wait_ge(s_chain, CH * (e + 1) + 7)
                    nc.tensor.matmul(ps_m[:, 0:C], k_act[:, :], w_t[:, 2, :], start=True, stop=True).then_inc(s_e8, 1)

            pe.sem_inc(s_tr, NBANKS)
            pe.sem_inc(s_pv, 2)
            for c in range(NPROJ):
                project(0, c, False)
                if c == 1:
                    pe.wait_ge(s_rpe_t, 2)
                    pe.wait_ge(s_const, 4)
                    for a in range(2):
                        ins = nc.tensor.matmul(ps_t[1][0:HEADS, :], rpe_t[:, a, :], upper[:, a, :],
                                               start=(a == 0), stop=(a == 1))
                    ins.then_inc(s_seq_mm, 1)
                if c % 2:
                    transpose_x(1 + c // 2)
            pe.wait_ge(s_in_w, 64)
            for a in range(3):
                ins = nc.tensor.transpose(ps_t[0][:, P * a:P * a + P], w_raw[:, a, :], ident[:, :])
            ins.then_inc(s_wt, 1)
            pe.wait_ge(s_xt, BATCH)
            pe.wait_ge(s_wt, 2)

            for r in range(LEAD):
                score(0, r)

            def step(n, prev, tile_too, more):
                for slot in range(NROWS):
                    for row in rows_ahead(n, more, slot):
                        score(*row)
                    if more and slot in PROJ_SLOTS:
                        project(n + 1, PROJ_SLOTS.index(slot), tile_too)
                    if tile_too:
                        tile_step(n, slot, more)
                    if prev and 0 <= slot - MIX_FAR < TILES:
                        mix(n - 1, 1, slot - MIX_FAR)
                    if 0 <= slot - MIX_NEAR < GROUP:
                        mix(n, 0, slot - MIX_NEAR)
                    transpose(n, slot)

            drive(pe, step)

            def out_project(w):
                for t in range(WIDE * w, WIDE * (w + 1)):
                    for p in range(PAIRS - 1):
                        ins = nc.tensor.matmul(ps_s[0][:, P * t:P * t + P], mix_last[:, p, P * t:P * t + P],
                                               wo[:, p, :], start=(p == 0), stop=(p == PAIRS - 2))
                ins.then_inc(last["out_projected"], 1)

            def project_last_pair(w):
                pe.wait_ge(s_o, 2 * (PAIR_STEPS - 1) + w + 2)
                for t in range(WIDE):
                    ins = nc.tensor.matmul(ps_s[1][:, P * (WIDE * w + t):P * (WIDE * w + t) + P],
                                           mix_sb[w][:, P * t:P * t + P], wo[:, PAIRS - 1, :], start=True, stop=True)
                ins.then_inc(last["pair_projected"], 1)

            def transpose_x1(w):
                pe.wait_ge(last["x1"], w + 1)
                for t in range(WIDE * w, WIDE * (w + 1)):
                    ins = nc.tensor.transpose(ps_s[1][:, P * t:P * t + P], x1_l[:, P * t:P * t + P], ident[:, :])
                ins.then_inc(last["x1_transposed"], 1)

            def project_rk(w):
                if w == 0:
                    for which in range(2):
                        pe.wait_ge(s_ev[which], EVACUATED[which] * (PAIR_STEPS + 1))
                pe.wait_ge(last["xrk"], w + 1)
                for t in range(WIDE * w, WIDE * (w + 1)):
                    nc.tensor.matmul(ps_s[0][:, P * t:P * t + P], xr_l[:, P * t:P * t + P], w_t[:, 0, :],
                                     start=True, stop=True)
                nc.tensor.matmul(ps_t[w][:, :], w_t[:, 1, :], xk_l[:, columns(w)], start=True, stop=True)\
                    .then_inc(last["rk_projected"], 1)

            def project_v(w):
                pe.wait_ge(last["k_squared"], w + 1)
                for t in range(WIDE * w, WIDE * (w + 1)):
                    ins = nc.tensor.matmul(ps_s[1][:, P * t:P * t + P], k_l[:, P * t:P * t + P], w_t[:, 2, :],
                                           start=True, stop=True)
                ins.then_inc(last["v_projected"], 1)

            tile_step(PAIR_STEPS, OUT_PROJ)
            pe.wait_ge(last["mix_loaded"], 32)
            pe.wait_ge(s_biased, NROWS * PAIR_STEPS + 2)
            out_project(0)
            project_last_pair(0)
            for j in range(TILES):
                mix(PAIR_STEPS - 1, 1, j)
            tile_step(PAIR_STEPS, X1_T)
            transpose_x1(0)
            out_project(1)
            project_last_pair(1)
            tile_step(PAIR_STEPS, RK_PROJ)
            project_rk(0)
            transpose_x1(1)
            tile_step(PAIR_STEPS, V_PROJ)
            project_v(0)
            project_rk(1)
            project_v(1)


_INS = ['L0_attn_x', 'L0_attn_qkv', 'L0_attn_out_w', 'L0_attn_rpe_bias', 'L0_ffn_W_r', 'L0_ffn_W_k', 'L0_ffn_W_v',
        'L0_ffn_mu_r', 'L0_ffn_mu_k']


def kernel(**inputs):
    import numpy as _np
    import concourse.bacc as _bacc
    from concourse import mybir as _mybir
    from concourse.bass_utils import run_bass_kernel_spmd as _run

    nc = _bacc.Bacc("TRN2", target_bir_lowering=False, num_devices=1)
    arrays, args = {}, []
    for name in _INS:
        a = _np.ascontiguousarray(inputs[name])
        arrays[f"in_{name}"] = a
        args.append(nc.dram_tensor(f"in_{name}", a.shape, _mybir.dt.from_np(a.dtype), kind="ExternalInput").ap())
    shape = inputs['L0_attn_x'].shape
    args.append(nc.dram_tensor("out_y", shape, _mybir.dt.float32, kind="ExternalOutput").ap())
    build(nc, *args)
    r = _run(nc, [arrays], core_ids=[0])
    return r.results[0]["out_y"]
```
